# Optimizing a Trainium2 kernel written in Bass

```python
import numpy as np
import jax
import jax.numpy as jnp

def _softmax(x, axis=-1):
    return jax.nn.softmax(x, axis=axis)

def _gelu(x):
    return jax.nn.gelu(x, approximate=True)

def _silu(x):
    return jax.nn.silu(x)

def _sigmoid(x):
    return jax.nn.sigmoid(x)

def _layernorm(x, axis=-1, eps=1e-05):
    m = jnp.mean(x, axis=axis, keepdims=True)
    v = jnp.var(x, axis=axis, keepdims=True)
    return (x - m) / jnp.sqrt(v + eps)

def _scatter_add(tgt, idx, src, axis=0):
    return tgt.at[idx].add(src)

def _segment_sum(src, seg, n):
    return jax.ops.segment_sum(src, seg, n)
kernel_name = 'mk_xattn_ffn_d2_seqx_r8_db80e4'

def setup_inputs(seed: int=0):
    np.random.seed(seed)
    _w = jnp.asarray

    def _rec_inputs():
        import jax
        import jax.numpy as jnp
        _rk = jax.random.key(seed)
        x = 7.22e-05 + 1 * jax.random.normal(jax.random.fold_in(_rk, 1), (4, 256, 256), jnp.float32)
        _lenS = 256 - jax.random.randint(jax.random.fold_in(_rk, 7), (4,), 0, max(1, 256 // 4) + 1, jnp.int32)
        _lenS2 = 64 - jax.random.randint(jax.random.fold_in(_rk, 8), (4,), 0, max(1, 64 // 4) + 1, jnp.int32)
        _ctx_2048P = jax.random.normal(jax.random.fold_in(_rk, 11), (4, 16, 256), jnp.float32)
        _ctx_2048c = jax.random.dirichlet(jax.random.fold_in(_rk, 511), 0.3 * jnp.ones((16,), jnp.float32), (4, 64))
        _ctx_2048t = jnp.einsum('bsk,bkd->bsd', _ctx_2048c, _ctx_2048P)
        _ctx_2048t = _ctx_2048t * jax.lax.rsqrt(jnp.mean(jnp.square(_ctx_2048t)) + 1e-12) * 0.953939
        ctx_2048 = 4.13588e-05 + 0.999923 * (_ctx_2048t + 0.3 * jax.random.normal(jax.random.fold_in(_rk, 611), (4, 64, 256), jnp.float32))
        return (x, ctx_2048)
    x, ctx_2048 = _rec_inputs()

    def _L0_xattn_setup():
        import math
        import jax, jax.numpy as jnp
        import numpy as np
        HEADS = 16
        MASKED_BIAS = -10000.0

        def _mha(q, k, v):
            B, Sq, D = q.shape
            Sk = k.shape[-2]
            hd = D // HEADS
            qh = q.reshape(B, Sq, HEADS, hd).transpose(0, 2, 1, 3)
            kh = k.reshape(B, Sk, HEADS, hd).transpose(0, 2, 1, 3)
            vh = v.reshape(B, Sk, HEADS, hd).transpose(0, 2, 1, 3)
            scores = jnp.einsum('bhqd,bhkd->bhqk', qh, kh) / math.sqrt(hd)
            qi = jnp.arange(Sq)[:, None] + (Sk - Sq)
            ki = jnp.arange(Sk)[None, :]
            causal = ki <= qi
            scores = jnp.where(causal[None, None], scores, jnp.asarray(MASKED_BIAS, scores.dtype))
            attn = jax.nn.softmax(scores, axis=-1)
            out = jnp.einsum('bhqk,bhkd->bhqd', attn, vh)
            return out.transpose(0, 2, 1, 3).reshape(B, Sq, D)
        key = jax.random.key(seed)
        kq, kk, kv = jax.random.split(key, 3)
        B, S, D = (4, 128, 256)
        q = jax.random.normal(kq, (B, S, D), dtype=jnp.float32)
        k = jax.random.normal(kk, (B, S, D), dtype=jnp.float32)
        v = jax.random.normal(kv, (B, S, D), dtype=jnp.float32)
        return {'q': q, 'k': k, 'v': v}
    _L0_xattn_all = _L0_xattn_setup()
    _L0_xattn_in = {k: v for k, v in _L0_xattn_all.items() if k in ()}
    del _L0_xattn_all

    def _L0_ffn_setup():
        import jax, jax.numpy as jnp
        import numpy as np
        EPS_NORM = 1e-06
        EPS_SCALE = 1e-05
        NUM_BITS = 8
        QP = 2 ** (NUM_BITS - 1) - 1
        QN = -2 ** (NUM_BITS - 1)

        def rms_norm(x, gamma):
            rms = jnp.sqrt(jnp.mean(x * x, axis=-1, keepdims=True) + EPS_NORM)
            return x / rms * gamma

        def activation_quant_8bit(x):
            scale = jnp.maximum(jnp.max(jnp.abs(x)), EPS_SCALE)
            x_scaled = x / scale * QP
            rounded = jnp.round(jnp.clip(x_scaled, QN, QP))
            x_quant = jax.lax.stop_gradient(rounded - x_scaled) + x_scaled
            return x_quant / QP * scale

        def weight_quant_ternary(w):
            scale = jnp.maximum(jnp.mean(jnp.abs(w)), EPS_SCALE)
            w_norm = w / scale
            w_q = jnp.round(jnp.clip(w_norm, -1.0, 1.0))
            return (jax.lax.stop_gradient(w_q - w_norm) + w_norm, scale)
        key = jax.random.key(seed)
        k1, k2 = jax.random.split(key)
        B, S, D_IN, D_OUT = (4, 512, 256, 256)
        x = jax.random.normal(k1, (B, S, D_IN), dtype=jnp.float32)
        bound = 1.0 / np.sqrt(D_IN)
        weight = jax.random.uniform(k2, (D_OUT, D_IN), dtype=jnp.float32, minval=-bound, maxval=bound)
        norm_weight = jnp.ones((D_IN,), dtype=jnp.float32)
        return {'x': x, 'weight': weight, 'norm_weight': norm_weight}
    _L0_ffn_all = _L0_ffn_setup()
    _L0_ffn_in = {k: v for k, v in _L0_ffn_all.items() if k in ('weight', 'norm_weight')}
    del _L0_ffn_all

    def _L1_xattn_setup():
        import jax, jax.numpy as jnp
        import numpy as np
        HIDDEN = 256
        NUM_HEADS = 16
        NUM_KV_HEADS = 4
        HEAD_DIM = 128
        ROPE_THETA = 10000.0
        EPS = 1e-06

        def rms_norm(x, w, eps=EPS):
            var = jnp.mean(jnp.square(x), axis=-1, keepdims=True)
            return x * jax.lax.rsqrt(var + eps) * w

        def rope_cache(L, head_dim, theta, dtype):
            inv_freq = 1.0 / theta ** (jnp.arange(0, head_dim, 2, dtype=jnp.float32) / head_dim)
            t = jnp.arange(L, dtype=jnp.float32)
            freqs = jnp.outer(t, inv_freq)
            emb = jnp.concatenate([freqs, freqs], -1)
            cos = jnp.cos(emb).astype(dtype)[None, :, None, :]
            sin = jnp.sin(emb).astype(dtype)[None, :, None, :]
            return (cos, sin)

        def rotate_half(x):
            x1, x2 = jnp.split(x, 2, axis=-1)
            return jnp.concatenate([-x2, x1], axis=-1)
        key = jax.random.key(seed)
        ks = jax.random.split(key, 10)
        B, L, T = (2, 256, 64)
        q_out = NUM_HEADS * HEAD_DIM
        kv_out = NUM_KV_HEADS * HEAD_DIM
        s = lambda fan_in: 1.0 / np.sqrt(fan_in)
        return {'x': jax.random.normal(ks[0], (B, L, HIDDEN), jnp.float32), 'h_ctx_kv': jax.random.normal(ks[1], (B, T, HIDDEN), jnp.float32), 'wq': jax.random.normal(ks[2], (HIDDEN, q_out), jnp.float32) * s(HIDDEN), 'wk': jax.random.normal(ks[3], (HIDDEN, kv_out), jnp.float32) * s(HIDDEN), 'wv': jax.random.normal(ks[4], (HIDDEN, kv_out), jnp.float32) * s(HIDDEN), 'wo': jax.random.normal(ks[5], (q_out, HIDDEN), jnp.float32) * s(q_out), 'wk_ctx': jax.random.normal(ks[6], (HIDDEN, kv_out), jnp.float32) * s(HIDDEN), 'wv_ctx': jax.random.normal(ks[7], (HIDDEN, kv_out), jnp.float32) * s(HIDDEN), 'q_norm_w': jnp.ones((HEAD_DIM,), jnp.float32), 'k_norm_w': jnp.ones((HEAD_DIM,), jnp.float32)}
    _L1_xattn_all = _L1_xattn_setup()
    _L1_xattn_in = {k: v for k, v in _L1_xattn_all.items() if k in ('wq', 'wk', 'wv', 'wo', 'wk_ctx', 'wv_ctx', 'q_norm_w', 'k_norm_w')}
    del _L1_xattn_all

    def _L1_ffn_setup():
        import jax, jax.numpy as jnp
        import numpy as np
        import math
        B, S, D = (2, 256, 256)
        H, HD = (16, 128)
        E, I = (4, 256)
        TOP_K = 2
        ROPE_THETA = 10000.0

        def _layernorm(x, w, b):
            mu = jnp.mean(x, axis=-1, keepdims=True)
            var = jnp.mean(jnp.square(x - mu), axis=-1, keepdims=True)
            return (x - mu) * jax.lax.rsqrt(var + 1e-05) * w + b

        def _rotate_half(x):
            x1, x2 = jnp.split(x, 2, axis=-1)
            return jnp.concatenate((-x2, x1), axis=-1)

        def _attention(h, wq, bq, wk, bk, wv, bv, wo, bo):
            b, s, _ = h.shape
            q = (h @ wq + bq).reshape(b, s, H, HD).transpose(0, 2, 1, 3)
            k = (h @ wk + bk).reshape(b, s, H, HD).transpose(0, 2, 1, 3)
            v = (h @ wv + bv).reshape(b, s, H, HD).transpose(0, 2, 1, 3)
            inv_freq = 1.0 / ROPE_THETA ** (jnp.arange(0, HD, 2, dtype=jnp.float32) / HD)
            freqs = jnp.arange(s, dtype=jnp.float32)[:, None] * inv_freq[None, :]
            emb = jnp.concatenate((freqs, freqs), axis=-1)
            cos = jnp.cos(emb)[None, None]
            sin = jnp.sin(emb)[None, None]
            q = q * cos + _rotate_half(q) * sin
            k = k * cos + _rotate_half(k) * sin
            scores = jnp.einsum('bhqd,bhkd->bhqk', q, k) / math.sqrt(HD)
            causal = jnp.tril(jnp.ones((s, s), bool))
            scores = jnp.where(causal[None, None], scores, jnp.finfo(jnp.float32).min)
            probs = jax.nn.softmax(scores.astype(jnp.float32), axis=-1).astype(q.dtype)
            out = jnp.einsum('bhqk,bhkd->bhqd', probs, v)
            out = out.transpose(0, 2, 1, 3).reshape(b, s, H * HD)
            return out @ wo + bo

        def _moe(h, w_gate, we1, be1, we2, be2):
            b, s, d = h.shape
            x = h.reshape(-1, d)
            t = x.shape[0]
            raw = jax.nn.softmax(x @ w_gate, axis=-1)
            top_vals, top_idx = jax.lax.top_k(raw, TOP_K)
            w = jax.nn.softmax(top_vals, axis=-1)
            comb = jnp.zeros((t, E), x.dtype).at[jnp.arange(t)[:, None], top_idx].add(w)
            hmid = jax.nn.gelu(jnp.einsum('td,edi->tei', x, we1) + be1[None], approximate=False)
            eout = jnp.einsum('tei,eid->ted', hmid, we2) + be2[None]
            out = jnp.einsum('te,ted->td', comb, eout)
            return out.reshape(b, s, d)
        key = jax.random.key(seed)
        ks = jax.random.split(key, 20)
        s = 0.02
        p = {'hidden_states': jax.random.normal(ks[0], (B, S, D), jnp.float32), 'wq': jax.random.normal(ks[1], (D, H * HD), jnp.float32) * s, 'bq': jnp.zeros((H * HD,), jnp.float32), 'wk': jax.random.normal(ks[2], (D, H * HD), jnp.float32) * s, 'bk': jnp.zeros((H * HD,), jnp.float32), 'wv': jax.random.normal(ks[3], (D, H * HD), jnp.float32) * s, 'bv': jnp.zeros((H * HD,), jnp.float32), 'wo': jax.random.normal(ks[4], (H * HD, D), jnp.float32) * s, 'bo': jnp.zeros((D,), jnp.float32), 'ln1_w': jnp.ones((D,), jnp.float32), 'ln1_b': jnp.zeros((D,), jnp.float32), 'ln2_w': jnp.ones((D,), jnp.float32), 'ln2_b': jnp.zeros((D,), jnp.float32), 'w_gate': jax.random.normal(ks[5], (D, E), jnp.float32) * s, 'we1': jax.random.normal(ks[6], (E, D, I), jnp.float32) * s, 'be1': jnp.zeros((E, I), jnp.float32), 'we2': jax.random.normal(ks[7], (E, I, D), jnp.float32) * s, 'be2': jnp.zeros((E, D), jnp.float32)}
        return p
    _L1_ffn_all = _L1_ffn_setup()
    _L1_ffn_in = {k: v for k, v in _L1_ffn_all.items() if k in ('wq', 'bq', 'wk', 'bk', 'wv', 'bv', 'wo', 'bo', 'ln1_w', 'ln1_b', 'ln2_w', 'ln2_b', 'w_gate', 'we1', 'be1', 'we2', 'be2')}
    del _L1_ffn_all
    return {'x': x, 'ctx_2048': ctx_2048, 'L0_ffn_weight': _L0_ffn_in['weight'], 'L0_ffn_norm_weight': _L0_ffn_in['norm_weight'], 'L1_xattn_wq': _L1_xattn_in['wq'], 'L1_xattn_wk': _L1_xattn_in['wk'], 'L1_xattn_wv': _L1_xattn_in['wv'], 'L1_xattn_wo': _L1_xattn_in['wo'], 'L1_xattn_wk_ctx': _L1_xattn_in['wk_ctx'], 'L1_xattn_wv_ctx': _L1_xattn_in['wv_ctx'], 'L1_xattn_q_norm_w': _L1_xattn_in['q_norm_w'], 'L1_xattn_k_norm_w': _L1_xattn_in['k_norm_w'], 'L1_ffn_wq': _L1_ffn_in['wq'], 'L1_ffn_bq': _L1_ffn_in['bq'], 'L1_ffn_wk': _L1_ffn_in['wk'], 'L1_ffn_bk': _L1_ffn_in['bk'], 'L1_ffn_wv': _L1_ffn_in['wv'], 'L1_ffn_bv': _L1_ffn_in['bv'], 'L1_ffn_wo': _L1_ffn_in['wo'], 'L1_ffn_bo': _L1_ffn_in['bo'], 'L1_ffn_ln1_w': _L1_ffn_in['ln1_w'], 'L1_ffn_ln1_b': _L1_ffn_in['ln1_b'], 'L1_ffn_ln2_w': _L1_ffn_in['ln2_w'], 'L1_ffn_ln2_b': _L1_ffn_in['ln2_b'], 'L1_ffn_w_gate': _L1_ffn_in['w_gate'], 'L1_ffn_we1': _L1_ffn_in['we1'], 'L1_ffn_be1': _L1_ffn_in['be1'], 'L1_ffn_we2': _L1_ffn_in['we2'], 'L1_ffn_be2': _L1_ffn_in['be2']}

def reference(x, ctx_2048, L0_ffn_weight, L0_ffn_norm_weight, L1_xattn_wq, L1_xattn_wk, L1_xattn_wv, L1_xattn_wo, L1_xattn_wk_ctx, L1_xattn_wv_ctx, L1_xattn_q_norm_w, L1_xattn_k_norm_w, L1_ffn_wq, L1_ffn_bq, L1_ffn_wk, L1_ffn_bk, L1_ffn_wv, L1_ffn_bv, L1_ffn_wo, L1_ffn_bo, L1_ffn_ln1_w, L1_ffn_ln1_b, L1_ffn_ln2_w, L1_ffn_ln2_b, L1_ffn_w_gate, L1_ffn_we1, L1_ffn_be1, L1_ffn_we2, L1_ffn_be2):
    import jax
    import jax.numpy as jnp

    def _L0_xattn_ref(q, k, v):
        import math
        import jax, jax.numpy as jnp
        import numpy as np
        HEADS = 16
        MASKED_BIAS = -10000.0

        def _mha(q, k, v):
            B, Sq, D = q.shape
            Sk = k.shape[-2]
            hd = D // HEADS
            qh = q.reshape(B, Sq, HEADS, hd).transpose(0, 2, 1, 3)
            kh = k.reshape(B, Sk, HEADS, hd).transpose(0, 2, 1, 3)
            vh = v.reshape(B, Sk, HEADS, hd).transpose(0, 2, 1, 3)
            scores = jnp.einsum('bhqd,bhkd->bhqk', qh, kh) / math.sqrt(hd)
            qi = jnp.arange(Sq)[:, None] + (Sk - Sq)
            ki = jnp.arange(Sk)[None, :]
            causal = ki <= qi
            scores = jnp.where(causal[None, None], scores, jnp.asarray(MASKED_BIAS, scores.dtype))
            attn = jax.nn.softmax(scores, axis=-1)
            out = jnp.einsum('bhqk,bhkd->bhqd', attn, vh)
            return out.transpose(0, 2, 1, 3).reshape(B, Sq, D)
        return _mha(q, k, v)

    def _L0_ffn_ref(x, weight, norm_weight):
        import jax, jax.numpy as jnp
        import numpy as np
        EPS_NORM = 1e-06
        EPS_SCALE = 1e-05
        NUM_BITS = 8
        QP = 2 ** (NUM_BITS - 1) - 1
        QN = -2 ** (NUM_BITS - 1)

        def rms_norm(x, gamma):
            rms = jnp.sqrt(jnp.mean(x * x, axis=-1, keepdims=True) + EPS_NORM)
            return x / rms * gamma

        def activation_quant_8bit(x):
            scale = jnp.maximum(jnp.max(jnp.abs(x)), EPS_SCALE)
            x_scaled = x / scale * QP
            rounded = jnp.round(jnp.clip(x_scaled, QN, QP))
            x_quant = jax.lax.stop_gradient(rounded - x_scaled) + x_scaled
            return x_quant / QP * scale

        def weight_quant_ternary(w):
            scale = jnp.maximum(jnp.mean(jnp.abs(w)), EPS_SCALE)
            w_norm = w / scale
            w_q = jnp.round(jnp.clip(w_norm, -1.0, 1.0))
            return (jax.lax.stop_gradient(w_q - w_norm) + w_norm, scale)
        xn = rms_norm(x, norm_weight)
        xq = activation_quant_8bit(xn)
        wq, w_scale = weight_quant_ternary(weight)
        out = jnp.einsum('bsi,oi->bso', xq, wq)
        return out * w_scale

    def _L1_xattn_ref(x, h_ctx_kv, wq, wk, wv, wo, wk_ctx, wv_ctx, q_norm_w, k_norm_w):
        import jax, jax.numpy as jnp
        import numpy as np
        HIDDEN = 256
        NUM_HEADS = 16
        NUM_KV_HEADS = 4
        HEAD_DIM = 128
        ROPE_THETA = 10000.0
        EPS = 1e-06

        def rms_norm(x, w, eps=EPS):
            var = jnp.mean(jnp.square(x), axis=-1, keepdims=True)
            return x * jax.lax.rsqrt(var + eps) * w

        def rope_cache(L, head_dim, theta, dtype):
            inv_freq = 1.0 / theta ** (jnp.arange(0, head_dim, 2, dtype=jnp.float32) / head_dim)
            t = jnp.arange(L, dtype=jnp.float32)
            freqs = jnp.outer(t, inv_freq)
            emb = jnp.concatenate([freqs, freqs], -1)
            cos = jnp.cos(emb).astype(dtype)[None, :, None, :]
            sin = jnp.sin(emb).astype(dtype)[None, :, None, :]
            return (cos, sin)

        def rotate_half(x):
            x1, x2 = jnp.split(x, 2, axis=-1)
            return jnp.concatenate([-x2, x1], axis=-1)
        B, L, _ = x.shape
        T = h_ctx_kv.shape[1]
        rep = NUM_HEADS // NUM_KV_HEADS
        q = (x @ wq).reshape(B, L, NUM_HEADS, HEAD_DIM)
        k = (x @ wk).reshape(B, L, NUM_KV_HEADS, HEAD_DIM)
        v = (x @ wv).reshape(B, L, NUM_KV_HEADS, HEAD_DIM)
        q = rms_norm(q, q_norm_w)
        k = rms_norm(k, k_norm_w)
        k_ctx = (h_ctx_kv @ wk_ctx).reshape(B, T, NUM_KV_HEADS, HEAD_DIM)
        v_ctx = (h_ctx_kv @ wv_ctx).reshape(B, T, NUM_KV_HEADS, HEAD_DIM)
        k_ctx = rms_norm(k_ctx, k_norm_w)
        cos, sin = rope_cache(L, HEAD_DIM, ROPE_THETA, x.dtype)
        q = q * cos + rotate_half(q) * sin
        k = k * cos + rotate_half(k) * sin
        k_full = jnp.concatenate([k_ctx, k], axis=1)
        v_full = jnp.concatenate([v_ctx, v], axis=1)
        k_full = jnp.repeat(k_full, rep, axis=2)
        v_full = jnpp_repeat = jnp.repeat(v_full, rep, axis=2)
        i = jnp.arange(L)[:, None]
        j = jnp.arange(L)[None, :]
        causal = jnp.where(j > i, -jnp.inf, 0.0).astype(x.dtype)
        mask = jnp.concatenate([jnp.zeros((L, T), x.dtype), causal], axis=1)
        scale = 1.0 / np.sqrt(HEAD_DIM)
        scores = jnp.einsum('blhd,bmhd->bhlm', q, k_full) * scale + mask
        probs = jax.nn.softmax(scores, axis=-1)
        out = jnp.einsum('bhlm,bmhd->blhd', probs, v_full)
        out = out.reshape(B, L, NUM_HEADS * HEAD_DIM)
        return out @ wo

    def _L1_ffn_ref(hidden_states, wq, bq, wk, bk, wv, bv, wo, bo, ln1_w, ln1_b, ln2_w, ln2_b, w_gate, we1, be1, we2, be2):
        import jax, jax.numpy as jnp
        import numpy as np
        import math
        B, S, D = (2, 256, 256)
        H, HD = (16, 128)
        E, I = (4, 256)
        TOP_K = 2
        ROPE_THETA = 10000.0

        def _layernorm(x, w, b):
            mu = jnp.mean(x, axis=-1, keepdims=True)
            var = jnp.mean(jnp.square(x - mu), axis=-1, keepdims=True)
            return (x - mu) * jax.lax.rsqrt(var + 1e-05) * w + b

        def _rotate_half(x):
            x1, x2 = jnp.split(x, 2, axis=-1)
            return jnp.concatenate((-x2, x1), axis=-1)

        def _attention(h, wq, bq, wk, bk, wv, bv, wo, bo):
            b, s, _ = h.shape
            q = (h @ wq + bq).reshape(b, s, H, HD).transpose(0, 2, 1, 3)
            k = (h @ wk + bk).reshape(b, s, H, HD).transpose(0, 2, 1, 3)
            v = (h @ wv + bv).reshape(b, s, H, HD).transpose(0, 2, 1, 3)
            inv_freq = 1.0 / ROPE_THETA ** (jnp.arange(0, HD, 2, dtype=jnp.float32) / HD)
            freqs = jnp.arange(s, dtype=jnp.float32)[:, None] * inv_freq[None, :]
            emb = jnp.concatenate((freqs, freqs), axis=-1)
            cos = jnp.cos(emb)[None, None]
            sin = jnp.sin(emb)[None, None]
            q = q * cos + _rotate_half(q) * sin
            k = k * cos + _rotate_half(k) * sin
            scores = jnp.einsum('bhqd,bhkd->bhqk', q, k) / math.sqrt(HD)
            causal = jnp.tril(jnp.ones((s, s), bool))
            scores = jnp.where(causal[None, None], scores, jnp.finfo(jnp.float32).min)
            probs = jax.nn.softmax(scores.astype(jnp.float32), axis=-1).astype(q.dtype)
            out = jnp.einsum('bhqk,bhkd->bhqd', probs, v)
            out = out.transpose(0, 2, 1, 3).reshape(b, s, H * HD)
            return out @ wo + bo

        def _moe(h, w_gate, we1, be1, we2, be2):
            b, s, d = h.shape
            x = h.reshape(-1, d)
            t = x.shape[0]
            raw = jax.nn.softmax(x @ w_gate, axis=-1)
            top_vals, top_idx = jax.lax.top_k(raw, TOP_K)
            w = jax.nn.softmax(top_vals, axis=-1)
            comb = jnp.zeros((t, E), x.dtype).at[jnp.arange(t)[:, None], top_idx].add(w)
            hmid = jax.nn.gelu(jnp.einsum('td,edi->tei', x, we1) + be1[None], approximate=False)
            eout = jnp.einsum('tei,eid->ted', hmid, we2) + be2[None]
            out = jnp.einsum('te,ted->td', comb, eout)
            return out.reshape(b, s, d)
        a = _attention(_layernorm(hidden_states, ln1_w, ln1_b), wq, bq, wk, bk, wv, bv, wo, bo)
        h = hidden_states + a
        m = _moe(_layernorm(h, ln2_w, ln2_b), w_gate, we1, be1, we2, be2)
        return h + m
    x = x + _L0_xattn_ref(_layernorm(x, axis=-1), ctx_2048, ctx_2048)
    x = x + _L0_ffn_ref(_layernorm(x, axis=-1), L0_ffn_weight, L0_ffn_norm_weight)
    x = x + _L1_xattn_ref(_layernorm(x, axis=-1), ctx_2048, L1_xattn_wq, L1_xattn_wk, L1_xattn_wv, L1_xattn_wo, L1_xattn_wk_ctx, L1_xattn_wv_ctx, L1_xattn_q_norm_w, L1_xattn_k_norm_w)
    x = x + _L1_ffn_ref(_layernorm(x, axis=-1), L1_ffn_wq, L1_ffn_bq, L1_ffn_wk, L1_ffn_bk, L1_ffn_wv, L1_ffn_bv, L1_ffn_wo, L1_ffn_bo, L1_ffn_ln1_w, L1_ffn_ln1_b, L1_ffn_ln2_w, L1_ffn_ln2_b, L1_ffn_w_gate, L1_ffn_we1, L1_ffn_be1, L1_ffn_we2, L1_ffn_be2)
    return x

_drawn_inputs = setup_inputs


def setup_inputs(seed=0):
    import zlib

    import numpy as np

    out = dict(_drawn_inputs(seed))
    spreads = {'L0_ffn_norm_weight': (1.0, 0.2),
     'L1_xattn_q_norm_w': (1.0, 0.545),
     'L1_xattn_k_norm_w': (1.0, 0.6),
     'L1_ffn_bq': (0.0, 0.8),
     'L1_ffn_bk': (0.0, 0.8),
     'L1_ffn_bv': (0.0, 0.1),
     'L1_ffn_bo': (0.0, 0.1),
     'L1_ffn_ln1_w': (1.0, 0.6),
     'L1_ffn_ln1_b': (0.0, 0.668),
     'L1_ffn_ln2_w': (1.0, 0.6),
     'L1_ffn_ln2_b': (0.0, 0.8),
     'L1_ffn_be1': (0.0, 0.8),
     'L1_ffn_be2': (0.0, 0.268)}
    factors = {'L1_ffn_wq': 8.0, 'L1_ffn_wk': 8.0, 'L1_ffn_we1': 3.357, 'L1_ffn_we2': 3.11}
    for name, (base, spread) in spreads.items():
        noise = np.random.default_rng([zlib.crc32(name.encode()), seed]).standard_normal(out[name].shape)
        drawn = base * np.exp(spread * noise) if base else spread * noise
        out[name] = jnp.asarray(drawn.astype(out[name].dtype))
    for name, factor in factors.items():
        out[name] = (out[name] * factor).astype(out[name].dtype)
    return out
```

```python
from contextlib import ExitStack

import concourse.bass as bass
import numpy as np
from concourse import mybir

F32 = mybir.dt.float32
F16 = mybir.dt.float16
BF16 = mybir.dt.bfloat16
ALU = mybir.AluOpType
ACT = mybir.ActivationFunctionType
AX = mybir.AxisListType
RMAX = bass.bass_isa.ReduceOp.max
RADD = bass.bass_isa.ReduceOp.add

P = 128
B, S, D = 4, 256, 256
NT = B * S // P
C = D // P
H, HD, G = 16, 128, 4
NCTX = 64
E = 4
WS = 256.0
NEG = -1e30
MEAN_SQ = 1.0 / (WS * HD ** 0.5)
MAGIC = 12582912.0
PASSES = ((0, 0), (0, 1), (1, 0))

_widths = dict(ident=128, causal=128, l0keep=64, l0fill=64, headsel=8, vsel=256, cos=256, sin=256)
CONST_AT, _at = {}, 0
for _name, _w in _widths.items():
    CONST_AT[_name] = (_at, _at + _w)
    _at += _w
NCONST = _at


def shape_constants():
    c = np.zeros((P, NCONST), np.float32)
    rows = np.arange(P)

    def put(name, v):
        a, b = CONST_AT[name]
        c[:, a:b] = v

    put("ident", np.eye(P))
    put("causal", np.where(rows[None, :] <= rows[:, None], 0.0, NEG))
    keep = np.arange(64)[None, :] <= (rows % 64)[:, None]
    put("l0keep", keep)
    put("l0fill", np.where(keep, 0.0, -10000.0))
    put("headsel", rows[:, None] // 16 == np.arange(8)[None, :])
    put("vsel", (np.arange(256)[None, :] // 16) % 2 == (rows // 64)[:, None])
    inv = (1.0 / np.power(np.float32(10000.0), np.arange(0, HD, 2, dtype=np.float32) / np.float32(HD)))
    ang = np.outer(np.arange(S, dtype=np.float32), inv.astype(np.float32)).astype(np.float32)
    cos, sin = np.cos(ang), np.sin(ang)
    for t in range(2):
        a = CONST_AT["cos"][0] + 128 * t
        c[:, a:a + 128] = np.concatenate([cos, cos], 1)[128 * t:128 * t + 128]
        a = CONST_AT["sin"][0] + 128 * t
        c[:, a:a + 128] = np.concatenate([-sin, sin], 1)[128 * t:128 * t + 128]
    return c


def done(eng, sem, count):
    if not (isinstance(count, int) and count <= 0):
        eng.wait_ge(sem, count)


def swap_halves(ap):
    return ap.rearrange("p t (a d) -> p t a d", a=2)[:, :, ::-1, :]


def halves(ap):
    return ap.rearrange("p t (a d) -> p t a d", a=2)


class Shared:
    pass


def build(nc, io, out):
    with ExitStack() as ctx:
        _build(nc, io, out, ctx)


def _build(nc, io, out, ctx):
    def sb(name, shape, dt=F32):
        return ctx.enter_context(nc.sbuf_tensor(name, shape, dt))

    layer_sems = []

    def sem(name):
        layer_sems.append(nc.alloc_semaphore(name=name))
        return layer_sems[-1]

    ps = ctx.enter_context(nc.psum_tensor("ps", [P, 8, 512], F32))
    psf = ps[:].rearrange("p a b -> p (a b)")

    def bank(i, lo=0, hi=512):
        return psf[:, 512 * i + lo:512 * i + hi]

    x = sb("x", [P, NT, D])
    h = sb("h", [P, NT, D])
    xn = sb("xn", [P, NT, D])
    hT = sb("hT", [P, 2, C, NT * P], F16)
    const = sb("const", [P, NCONST])
    w_xq_moe = sb("w_xq_moe", [P, 2, 4096], F16)
    w_xkv = sb("w_xkv", [P, 2, C, 2, 2, 512], F16)
    w_xo = sb("w_xo", [P, 2, H, D], F16)
    w_fqkv = sb("w_fqkv", [P, 2, C, 3, 2048], F16)
    w_fo = sb("w_fo", [P, 2, H, D], F16)
    piece = sb("piece", [P, 4, 256])
    stats = sb("stats", [P, NT, 6])
    meanvar = sb("meanvar", [P, NT, 2])
    rstd = sb("rstd", [P, NT])
    neg_half = sb("neg_half", [P, NT])
    ctxT = sb("ctxT", [P, 2, C, B, P], F16)
    ws_row = sb("ws_row", [P, 256])
    ident_bf = sb("ident_bf", [P, P], BF16)
    causal_bf = sb("causal_bf", [P, P], BF16)
    neg_max = sb("neg_max", [P, 2, 2])
    exp_bias = sb("exp_bias", [P, 2, 2])
    row_sum = sb("row_sum", [P, 2, 2])
    inv_sum = sb("inv_sum", [P, 2, 2])
    prob = sb("prob", [P, 2, 512])
    probT = sb("probT", [P, 2, 2, 512], F16)
    oT = sb("oT", [P, 2, 2, 256], F16)
    qkT = sb("qkT", [P, 2, 2, 512], F16)
    qk_raw = sb("qk_raw", [P, 2, 2, 256])
    ln_full = qk_raw[:].rearrange("p a t d -> p a (t d)")
    rope_a = sb("rope_a", [P, 2, 2, 256])
    rope_b = sb("rope_b", [P, 2, 2, 256])
    tab_cos = sb("tab_cos", [P, 2, 2, 128])
    tab_sin = sb("tab_sin", [P, 2, 2, 128])
    small = sb("small", [P, 64])
    fcols = sb("fcols", [P, 64])
    vpair = sb("vpair", [P, 2, 2, 4, 128], F16)
    kT = sb("kT", [P, 2, 2, 320], F16)

    def cst(name):
        a, b = CONST_AT[name]
        return const[:, a:b]

    ident = cst("ident")
    scratch = w_fqkv[:].rearrange("p a c k n -> p (a c k n)")
    scratch32 = scratch.bitcast(F32)
    stage32 = w_fo[:].rearrange("p a h d -> p (a h d)").bitcast(F32)
    w_xq = w_xq_moe[:].rearrange("p a (c n) -> p a c n", c=C)

    def groups_of(tiles):
        return [tiles[i:i + 4] for i in range(0, len(tiles), 4)]

    def columns(group):
        return slice(group[0], group[-1] + 1, group[1] - group[0])

    def ln_stats(dve, ln, tiles, x=x):
        for g, group in enumerate(groups_of(tiles)):
            for T in group:
                nc.vector.bn_stats(stats[:, T, :], x[:, T, :]).then_inc(ln["stats"], 1)
            for i, T in enumerate(group):
                dve.wait_ge(ln["stats"], 4 * g + i + 1)
                nc.vector.bn_aggr(meanvar[:, T, :], stats[:, T, :]).then_inc(ln["var"], 1)
            dve.wait_ge(ln["var"], 4 * g + 4)
            nc.vector.tensor_scalar(rstd[:, columns(group)], meanvar[:, columns(group), 1], 1e-5, None,
                                    ALU.add).then_inc(ln["eps"], 1)

    def ln_rstd(pool, ln, tiles):
        for g, group in enumerate(groups_of(tiles)):
            pool.wait_ge(ln["eps"], g + 1)
            sel = columns(group)
            nc.gpsimd.tensor_tensor(rstd[:, sel], rstd[:, sel], neg_half[:, sel], ALU.pow).then_inc(ln["rstd"], 1)

    def ln_apply(dve, ln, tiles, x=x):
        for g, group in enumerate(groups_of(tiles)):
            dve.wait_ge(ln["rstd"], g + 1)
            for T in group:
                nc.vector.tensor_scalar(xn[:, T, :], x[:, T, :], meanvar[:, T, 0:1], rstd[:, T:T + 1],
                                        ALU.subtract, ALU.mult).then_inc(ln["xn"], 1)

    def ln_turn(pe, ln, tiles, first_bank):
        for i, T in enumerate(tiles):
            pe.wait_ge(ln["xn"], i + 1)
            for c in range(C):
                at = first_bank + C * (i // 4) + c
                last = nc.tensor.transpose(bank(at, P * (i % 4), P * (i % 4) + P),
                                           xn[:, T, c * P:(c + 1) * P], ident)
            last.then_inc(ln["xT"], 1)

    def ln_hi(act, ln, first_bank, groups, scale=None, shift=None):
        for g in range(groups):
            act.wait_ge(ln["xT"], 4 * g + 4)
            for c in range(C):
                src, dst = bank(first_bank + C * g + c), hT[:, 0, c, 512 * g:512 * g + 512]
                if scale is None:
                    nc.scalar.activation(dst, src, ACT.Copy).then_inc(ln["hi"], 1)
                    continue
                nc.scalar.activation(dst, src, ACT.Identity, scale=scale[:, c:c + 1],
                                     bias=shift[:, c:c + 1]).then_inc(ln["hi"], 1)
                if c == 1:
                    done(act, ln["lo"], C * g)
                    nc.scalar.activation(ln_full[:, 1], src, ACT.Identity, scale=scale[:, c:c + 1],
                                         bias=shift[:, c:c + 1]).then_inc(ln["full1"], 1)

    def ln_lo(dve, ln, first_bank, groups, scale=None, shift=None):
        for g in range(groups):
            dve.wait_ge(ln["xT"], 4 * g + 4)
            for c in range(C):
                k = C * g + c
                src, cols = bank(first_bank + k), slice(512 * g, 512 * g + 512)
                dve.wait_ge(ln["hi"], k + 1)
                if scale is not None:
                    if c == 0:
                        nc.vector.tensor_scalar(ln_full[:, 0], src, scale[:, c:c + 1], shift[:, c:c + 1],
                                                ALU.mult, ALU.add).then_inc(ln["full"], 1)
                    dve.wait_ge(ln["full1" if c else "full"], g + 1)
                    src = ln_full[:, c]
                nc.vector.tensor_tensor(hT[:, 1, c, cols], src, hT[:, 0, c, cols],
                                        ALU.subtract).then_inc(ln["lo"], 1)
            if scale is not None:
                dve.wait_ge(ln["lo"], C * (g + 1))

    def ln_sems(tag):
        return {k: sem(f"{tag}_{k}") for k in ("stats", "var", "eps", "rstd", "xn", "xT", "hi", "full", "full1", "lo")}

    m = Shared()
    m.bank = bank
    m.causal_bf = causal_bf
    m.const = const
    m.cst = cst
    m.ctxT = ctxT
    m.exp_bias = exp_bias
    m.fcols = fcols
    m.h = h
    m.hT = hT
    m.ident = ident
    m.ident_bf = ident_bf
    m.inv_sum = inv_sum
    m.io = io
    m.kT = kT
    m.ln_apply = ln_apply
    m.ln_hi = ln_hi
    m.ln_lo = ln_lo
    m.ln_rstd = ln_rstd
    m.ln_sems = ln_sems
    m.ln_stats = ln_stats
    m.ln_turn = ln_turn
    m.meanvar = meanvar
    m.neg_half = neg_half
    m.neg_max = neg_max
    m.oT = oT
    m.out = out
    m.piece = piece
    m.prob = prob
    m.probT = probT
    m.psf = psf
    m.qkT = qkT
    m.qk_raw = qk_raw
    m.rope_a = rope_a
    m.rope_b = rope_b
    m.row_sum = row_sum
    m.rstd = rstd
    m.scratch = scratch
    m.scratch32 = scratch32
    m.sem = sem
    m.small = small
    m.stage32 = stage32
    m.tab_cos = tab_cos
    m.tab_sin = tab_sin
    m.vpair = vpair
    m.w_fo = w_fo
    m.w_fqkv = w_fqkv
    m.w_xkv = w_xkv
    m.w_xo = w_xo
    m.w_xq = w_xq
    m.w_xq_moe = w_xq_moe
    m.ws_row = ws_row
    m.x = x
    m.xn = xn
    for part in PARTS:
        part(nc, m)
        nc.clear_and_free_semaphores(layer_sems)
        nc.all_engine_barrier()
        layer_sems.clear()


def layer0_attention(nc, m):
    P64 = 64
    odd = [1, 3, 5, 7]
    x, xn, hT, const, small, sem, bank, scratch, scratch32 = (
        m.x, m.xn, m.hT, m.const, m.small, m.sem, m.bank, m.scratch, m.scratch32)
    keyT_bd = scratch[:, 0:8192].rearrange("p (a c b h k) -> p a c b h k", a=2, c=C, b=B, h=8)
    probT0 = scratch[:, 8192:12288].rearrange("p (a s h n) -> p a s h n", a=2, s=2, h=8)
    ctx_pair = scratch[:, 12288:14336].rearrange("p (a b d) -> p a b d", a=2, b=B)
    val_bd = scratch[:, 14336:16384].rearrange("p (a b d) -> p a b d", a=2, b=B)
    inv_keys = scratch[:, 16384:16384 + P]
    ctx_rows = scratch32[:, 8320:9344].rearrange("p (b d) -> p b d", b=B)
    score = xn[:].rearrange("p t d -> p (t d)").rearrange("p (s h k) -> p s h k", s=2, h=16)
    hmax = small[:, 0:32].rearrange("p (s h) -> p s h", s=2)
    hsum = small[:, 32:64].rearrange("p (s h) -> p s h", s=2)
    ln = m.ln_sems("a0")
    s_x, s_const, s_ctx, s_fill = sem("s_x"), sem("s_const"), sem("s_ctx"), sem("s_fill")
    s_stage = [sem(f"s_stage{i}") for i in range(6)]
    s_wfull, s_whi, s_wlo, s_wlast = sem("s_wfull"), sem("s_whi"), sem("s_wlo"), sem("s_wlast")
    ctx_turned, ctxT_hi, ctxT_lo, keys_bd = sem("ctx_turned"), sem("ctxT_hi"), sem("ctxT_lo"), sem("keys_bd")
    ctx_hi, ctx_lo, vals_bd = sem("ctx_hi"), sem("ctx_lo"), sem("vals_bd")
    scored, masked, maxed, shifted = sem("scored0"), sem("masked0"), sem("maxed0"), sem("shifted0")
    exped, summed, normed = sem("exped0"), sem("summed0"), sem("normed0")
    prob_turned, probT_hi, probT_lo = sem("prob_turned0"), sem("probT_hi0"), sem("probT_lo0")
    attended, meaned, added = sem("attended0"), sem("meaned0"), sem("added0")

    stage = [m.stage32[:, 0:2048], m.stage32[:, 2048:4096], scratch32[:, 9344:11392],
             m.h[:].rearrange("p t d -> p (t d)")]
    wx = {k: m.io["L1_xattn_" + k] for k in ("wq", "wk", "wv", "wk_ctx", "wv_ctx", "wo")}
    wo_rows = wx["wo"].rearrange("(h p) d -> p h d", p=P)
    pieces = []
    for c in range(C):
        pieces.append(([(0, 2048, wx["wq"][c * P:(c + 1) * P, :])], m.w_xq[:, :, c, :]))
    for c in range(C):
        loads = [(512 * i, 512, wx[k][c * P:(c + 1) * P, :]) for i, k in enumerate(("wk", "wv", "wk_ctx", "wv_ctx"))]
        pieces.append((loads, m.w_xkv[:, :, c].rearrange("p a s k n -> p a (s k n)")))
    for i in range(2):
        pieces.append(([(0, 2048, wo_rows[:, 8 * i:8 * i + 8, :])],
                       m.w_xo[:, :, 8 * i:8 * i + 8, :].rearrange("p a h d -> p a (h d)")))

    def head_keys(eng, ops, hl, c):
        eng.wait_ge(s_const, 16)
        eng.wait_ge(ctxT_hi if hl == 0 else ctxT_lo, 2)
        keys = m.ctxT[:, hl, c, :, P64:].unsqueeze(2).broadcast_to([P, B, 8, P64])
        sel = m.cst("headsel").unsqueeze(1).unsqueeze(3).broadcast_to([P, B, 8, P64])
        ops.tensor_tensor(keyT_bd[:, hl, c], keys, sel, ALU.mult).then_inc(keys_bd, 1)

    with nc.Block() as block:

        @block.sync
        def _(sp):
            sp.dma_start(x[:], m.io["x"].rearrange("b (t p) d -> p (b t) d", p=P)).then_inc(s_x, 16)
            sp.dma_start(const[:], m.io["const"]).then_inc(s_const, 16)
            keys = m.io["ctx_2048"].rearrange("b k d -> k b d")
            for half in range(2):
                sp.dma_start(ctx_rows[64 * half:64 * half + 64], keys).then_inc(s_ctx, 16)
            for i, (loads, _dst) in enumerate(pieces):
                if i >= 4:
                    sp.wait_ge(s_wlo, i - 3)
                for a, n, src in loads:
                    dst = stage[i % 4][:, a:a + n]
                    if len(src.shape) == 3:
                        dst = dst.rearrange("p (h d) -> p h d", d=D)
                    sp.dma_start(dst, src).then_inc(s_stage[i], 16)

        @block.gpsimd
        def _(pool):
            nc.gpsimd.memset(m.neg_half[:], -0.5).then_inc(s_fill, 1)
            nc.gpsimd.memset(inv_keys, 1.0 / P).then_inc(s_fill, 1)
            nc.gpsimd.memset(m.ws_row[:], WS).then_inc(s_fill, 1)
            nc.gpsimd.memset(m.vpair[:], 0.0)
            pool.wait_ge(s_fill, 3)
            m.ln_rstd(pool, ln, odd)
            head_keys(pool, nc.gpsimd, 1, 1)
            for i, (_loads, dst) in enumerate(pieces[:-1]):
                pool.wait_ge(s_whi, i + 1)
                nc.gpsimd.tensor_tensor(dst[:, 1], stage[i % 4], dst[:, 0], ALU.subtract).then_inc(s_wlo, 1)

        @block.tensor
        def _(pe):
            pe.wait_ge(s_ctx, 32)
            pe.wait_ge(s_const, 16)
            for c in range(C):
                for b in range(B):
                    at = P64 * (B * c + b)
                    last = nc.tensor.transpose(bank(2, at, at + P64), ctx_rows[0:P64, b, c * P:(c + 1) * P],
                                               m.ident[0:P64, 0:P64])
            last.then_inc(ctx_turned, 1)
            m.ln_turn(pe, ln, odd, 0)
            pe.wait_ge(ctx_hi, 1)
            pe.wait_ge(ctx_lo, 1)
            pe.wait_ge(s_fill, 3)
            for half in range(2):
                for hl in range(2):
                    last = nc.tensor.matmul(bank(3 + half), inv_keys, ctx_pair[:, hl, 2 * half:2 * half + 2, :],
                                            start=(hl == 0), stop=(hl == 1))
            last.then_inc(meaned, 1)
            for s in range(2):
                if s == 0:
                    pe.wait_ge(ln["lo"], 2)
                    pe.wait_ge(keys_bd, 4)
                else:
                    pe.wait_ge(masked, 1)
                for c in range(C):
                    for b in (2 * s, 2 * s + 1):
                        at = P64 * (b % 2)
                        for i, (a, w) in enumerate(PASSES):
                            last = nc.tensor.matmul(bank(5 + c)[at:at + P64], hT[:, a, c, P * b + P64:P * b + P],
                                                    keyT_bd[:, w, c, b], start=(i == 0), stop=(i == 2))
                last.then_inc(scored, 1)
            for s in range(2):
                pe.wait_ge(normed, s + 1)
                if s == 1:
                    pe.wait_ge(probT_lo, 1)
                for hp in range(8):
                    last = nc.tensor.transpose(bank(hp // 4, P * (hp % 4), P * (hp % 4) + P),
                                               score[:, s, 2 * hp:2 * hp + 2, :], m.ident)
                last.then_inc(prob_turned, 1)
            pe.wait_ge(vals_bd, 2)
            for s in range(2):
                pe.wait_ge(probT_lo, s + 1)
                for b in (2 * s, 2 * s + 1):
                    at = P64 * (b % 2)
                    for hp in range(8):
                        for i, (a, w) in enumerate(PASSES):
                            last = nc.tensor.matmul(bank(7, 256 * s + 32 * hp, 256 * s + 32 * hp + 32)[at:at + P64],
                                                    probT0[:, a, s, hp, at:at + P64],
                                                    val_bd[:, w, b, 32 * hp:32 * hp + 32],
                                                    start=(i == 0), stop=(i == 2))
                last.then_inc(attended, 1)

        @block.scalar
        def _(act):
            act.wait_ge(s_ctx, 32)
            nc.scalar.activation(ctx_pair[:, 0], ctx_rows, ACT.Copy).then_inc(ctx_hi, 1)
            act.wait_ge(ctx_turned, 1)
            act.wait_ge(s_fill, 3)
            src = bank(2).rearrange("p (c b k) -> p c b k", c=C, b=B)
            for c in range(C):
                nc.scalar.activation(m.ctxT[:, 0, c].rearrange("p b (r k) -> p b r k", r=2),
                                     src[:, c].unsqueeze(2).broadcast_to([P, B, 2, P64]), ACT.Copy).then_inc(ctxT_hi, 1)
            m.ln_hi(act, ln, 0, 1)
            act.wait_ge(ctxT_lo, 2)
            for h in range(8):
                last = nc.scalar.activation(keyT_bd[:, 1, 0, :, h, :], m.ctxT[:, 1, 0, :, P64:], ACT.Copy,
                                            scale=m.cst("headsel")[:, h:h + 1])
            last.then_inc(keys_bd, 1)

            def weight(i):
                loads, dst = pieces[i]
                act.wait_ge(s_stage[i], 16 * len(loads))
                w = stage[i % 4]
                nc.scalar.activation(w, w, ACT.Copy, scale=WS).then_inc(s_wfull, 1)
                act.wait_ge(s_wfull, i + 1)
                nc.scalar.activation(dst[:, 0], w, ACT.Copy).then_inc(s_whi, 1)

            def exponent(s):
                act.wait_ge(shifted, s + 1)
                nc.scalar.activation(score[:, s], score[:, s], ACT.Exp).then_inc(exped, 1)

            def prob_hi(s):
                act.wait_ge(prob_turned, s + 1)
                nc.scalar.activation(probT0[:, 0, s].rearrange("p h n -> p (h n)"), m.psf[:, 0:1024],
                                     ACT.Copy).then_inc(probT_hi, 1)

            weight(0)
            weight(1)
            exponent(0)
            weight(2)
            exponent(1)
            weight(3)
            prob_hi(0)
            weight(4)
            prob_hi(1)
            weight(5)

        @block.vector
        def _(dve):
            dve.wait_ge(s_x, 16)
            m.ln_stats(dve, ln, odd)
            dve.wait_ge(s_const, 16)
            nc.vector.tensor_copy(m.ident_bf[:], m.ident)
            nc.vector.tensor_copy(m.causal_bf[:], m.cst("causal"))
            dve.wait_ge(ctx_hi, 1)
            dve.wait_ge(s_ctx, 32)
            nc.vector.tensor_tensor(ctx_pair[:, 1], ctx_rows, ctx_pair[:, 0], ALU.subtract).then_inc(ctx_lo, 1)
            m.ln_apply(dve, ln, odd)
            src = bank(2).rearrange("p (c b k) -> p c b k", c=C, b=B)
            for c in range(C):
                dve.wait_ge(ctxT_hi, 2)
                nc.vector.tensor_tensor(m.ctxT[:, 1, c].rearrange("p b (r k) -> p b r k", r=2),
                                        src[:, c].unsqueeze(2).broadcast_to([P, B, 2, P64]),
                                        m.ctxT[:, 0, c].rearrange("p b (r k) -> p b r k", r=2),
                                        ALU.subtract).then_inc(ctxT_lo, 1)
            head_keys(dve, nc.vector, 0, 0)
            head_keys(dve, nc.vector, 0, 1)
            m.ln_lo(dve, ln, 0, 1)
            dve.wait_ge(ctx_lo, 1)
            for hl in range(2):
                sel = m.cst("vsel").unsqueeze(1).broadcast_to([P, B, D])
                nc.vector.tensor_tensor(val_bd[:, hl], ctx_pair[:, hl], sel, ALU.mult).then_inc(vals_bd, 1)
            for s in range(2):
                dve.wait_ge(scored, s + 1)
                if s == 0:
                    dve.wait_ge(ln["xT"], 4)
                raw = m.psf[:, 512 * 5:512 * 7].rearrange("p (h k) -> p h k", k=P64)
                keep = m.cst("l0keep").unsqueeze(1).broadcast_to([P, 16, P64])
                fill = m.cst("l0fill").unsqueeze(1).broadcast_to([P, 16, P64])
                nc.vector.scalar_tensor_tensor(out=score[:, s], in0=raw, scalar=0.25, in1=keep,
                                               op0=ALU.mult, op1=ALU.mult).then_inc(masked, 1)
                dve.wait_ge(masked, s + 1)
                nc.vector.tensor_tensor(score[:, s], score[:, s], fill, ALU.add).then_inc(maxed, 1)
                dve.wait_ge(maxed, 2 * s + 1)
                nc.vector.tensor_reduce(hmax[:, s], score[:, s], AX.X, ALU.max).then_inc(maxed, 1)
                dve.wait_ge(maxed, 2 * s + 2)
                nc.vector.tensor_tensor(score[:, s], score[:, s],
                                        hmax[:, s].unsqueeze(2).broadcast_to([P, 16, P64]),
                                        ALU.subtract).then_inc(shifted, 1)
            for s in range(2):
                dve.wait_ge(exped, s + 1)
                nc.vector.tensor_reduce(hsum[:, s], score[:, s], AX.X, ALU.add).then_inc(summed, 1)
                dve.wait_ge(summed, 2 * s + 1)
                nc.vector.reciprocal(hsum[:, s], hsum[:, s]).then_inc(summed, 1)
                dve.wait_ge(summed, 2 * s + 2)
                nc.vector.tensor_tensor(score[:, s], score[:, s],
                                        hsum[:, s].unsqueeze(2).broadcast_to([P, 16, P64]),
                                        ALU.mult).then_inc(normed, 1)
            def prob_lo(s):
                dve.wait_ge(probT_hi, s + 1)
                nc.vector.tensor_tensor(probT0[:, 1, s].rearrange("p h n -> p (h n)"), m.psf[:, 0:1024],
                                        probT0[:, 0, s].rearrange("p h n -> p (h n)"),
                                        ALU.subtract).then_inc(probT_lo, 1)

            prob_lo(0)
            dve.wait_ge(meaned, 1)
            mean = m.psf[:, 512 * 3:512 * 5].rearrange("p (b d) -> p b d", b=B)
            xt = x[:].rearrange("p (b t) d -> p b t d", t=2)
            nc.vector.tensor_tensor(xt[:, :, 0], mean, xt[:, :, 0], ALU.add).then_inc(added, 1)
            nc.vector.tensor_tensor(xt[0:64, :, 1], mean[0:64], xt[0:64, :, 1], ALU.add).then_inc(added, 1)
            prob_lo(1)
            last = len(pieces) - 1
            dve.wait_ge(s_whi, last + 1)
            nc.vector.tensor_tensor(pieces[last][1][:, 1], stage[last % 4], pieces[last][1][:, 0],
                                    ALU.subtract).then_inc(s_wlast, 1)
            dve.wait_ge(attended, 2)
            for b in range(B):
                at = P64 * (b % 2)
                nc.vector.tensor_tensor(xt[64:128, b, 1], bank(7, 256 * (b // 2), 256 * (b // 2) + 256)[at:at + P64],
                                        xt[64:128, b, 1], ALU.add).then_inc(added, 1)


def layer0_ffn(nc, m):
    x, xn, small, sem, bank, psf = m.x, m.xn, m.small, m.sem, m.bank, m.psf
    tiles = list(range(NT))
    full = m.scratch32[:, 0:2048].rearrange("p (c n) -> p c n", c=C)
    quant = m.scratch[:, 4096:6144].rearrange("p (c n) -> p c n", c=C)
    wrow = m.scratch32[:, 3072:3584].rearrange("p (o i) -> p o i", o=2)
    wT = m.scratch[:, 7168:7680].rearrange("p (c o) -> p c o", c=C)
    gamma = m.fcols[:, 0:2]
    xabs, xmax, xinv, wabs, wsum, wscale, winv, outscale = (small[:, i:i + 1] for i in range(8))
    rms, xabs4 = small[:, 8:16], small[:, 16:20]
    ln = m.ln_sems("f0")
    s_w, s_gamma = sem("f0_w"), sem("f0_gamma")
    wsummed, wall, wprep, wq, w_turned, w_ready = (sem("f0_" + k) for k in ("wsummed", "wall", "wprep", "wq", "w_turned", "w_ready"))
    rms_done, scaled, gained, xabsed, xall, xprep, quanted = (
        sem("f0_" + k) for k in ("rms", "scaled", "gained", "xabs", "xall", "xprep", "quant"))
    xabsed4, multiplied, added = sem("f0_xabs4"), sem("f0_mm"), sem("f0_added")

    with nc.Block() as block:

        @block.sync
        def _(sp):
            sp.dma_start(wrow, m.io["L0_ffn_weight"].rearrange("(o p) i -> p o i", p=P)).then_inc(s_w, 16)
            with nc.allow_non_contiguous_dma(reason="256 numbers, one per partition"):
                sp.dma_start(gamma, m.io["L0_ffn_norm_weight"].rearrange("(c p) -> p c", p=P)).then_inc(s_gamma, 16)

        @block.gpsimd
        def _(pool):
            pool.wait_ge(rms_done, 1)
            nc.gpsimd.tensor_tensor(m.rstd[:], rms, m.neg_half[:], ALU.pow).then_inc(scaled, 1)
            pool.wait_ge(wsummed, 1)
            nc.gpsimd.partition_all_reduce(wsum, wabs, P, RADD).then_inc(wall, 1)
            pool.wait_ge(xabsed, 1)
            nc.gpsimd.partition_all_reduce(xmax, xabs, P, RMAX).then_inc(xall, 1)

        @block.vector
        def _(dve):
            m.ln_stats(dve, ln, tiles)
            dve.wait_ge(ln["var"], NT)
            nc.vector.tensor_scalar(rms, m.meanvar[:, :, 1], 1.0 + 1e-6, 1e-11, ALU.mult, ALU.add).then_inc(rms_done, 1)
            dve.wait_ge(s_w, 16)
            nc.vector.tensor_reduce(wabs, wrow, AX.XY, ALU.add, apply_absolute_value=True).then_inc(wsummed, 1)
            dve.wait_ge(scaled, 1)
            for T in tiles:
                nc.vector.tensor_scalar(xn[:, T, :], x[:, T, :], m.meanvar[:, T, 0:1], m.rstd[:, T:T + 1],
                                        ALU.subtract, ALU.mult).then_inc(ln["xn"], 1)
            dve.wait_ge(wall, 1)
            nc.vector.tensor_scalar(wscale, wsum, 1.0 / (D * D), 1e-5, ALU.mult, ALU.max).then_inc(wprep, 1)
            dve.wait_ge(wprep, 1)
            nc.vector.reciprocal(winv, wscale).then_inc(wprep, 1)
            dve.wait_ge(wprep, 2)
            nc.vector.tensor_scalar(wrow, wrow, winv, -1.0, ALU.mult, ALU.max).then_inc(wprep, 1)
            dve.wait_ge(wprep, 3)
            nc.vector.tensor_scalar(wrow, wrow, 1.0, MAGIC, ALU.min, ALU.add).then_inc(wprep, 1)
            dve.wait_ge(wprep, 4)
            nc.vector.tensor_scalar(wrow, wrow, MAGIC, None, ALU.subtract).then_inc(wq, 1)
            for k in range(4):
                g, c = k // 2, k % 2
                dve.wait_ge(gained, k + 1)
                nc.vector.tensor_reduce(xabs4[:, k:k + 1], full[:, c, 512 * g:512 * g + 512], AX.X, ALU.max,
                                        apply_absolute_value=True).then_inc(xabsed4, 1)
            dve.wait_ge(xabsed4, 4)
            nc.vector.tensor_reduce(xabs, xabs4, AX.X, ALU.max).then_inc(xabsed, 1)
            dve.wait_ge(xall, 1)
            nc.vector.tensor_scalar(xmax, xmax, 1e-5, None, ALU.max).then_inc(xprep, 1)
            dve.wait_ge(xprep, 1)
            nc.vector.reciprocal(xinv, xmax).then_inc(xprep, 1)
            nc.vector.tensor_scalar(outscale, xmax, wscale, 1.0 / 127.0, ALU.mult, ALU.mult).then_inc(xprep, 1)
            dve.wait_ge(xprep, 3)
            for g in range(2):
                half = full[:, :, 512 * g:512 * g + 512]
                nc.vector.tensor_scalar(half, half, xinv, 127.0, ALU.mult, ALU.mult).then_inc(xprep, 1)
                dve.wait_ge(xprep, 2 * g + 4)
                nc.vector.tensor_scalar(half, half, 127.0, -128.0, ALU.min, ALU.max).then_inc(xprep, 1)
                dve.wait_ge(xprep, 2 * g + 5)
                nc.vector.tensor_scalar(quant[:, :, 512 * g:512 * g + 512], half, MAGIC, MAGIC,
                                        ALU.add, ALU.subtract).then_inc(quanted, 1)
            for g in range(4):
                dve.wait_ge(multiplied, g + 1)
                rows = x[:, 2 * g:2 * g + 2, :].rearrange("p t d -> p (t d)")
                nc.vector.scalar_tensor_tensor(out=rows, in0=bank(4 + g), scalar=outscale, in1=rows,
                                               op0=ALU.mult, op1=ALU.add).then_inc(added, 1)

        @block.tensor
        def _(pe):
            m.ln_turn(pe, ln, tiles, 0)
            pe.wait_ge(wq, 1)
            for o in range(2):
                for c in range(C):
                    last = nc.tensor.transpose(bank(4, 256 * c + P * o, 256 * c + P * o + P),
                                               wrow[:, o, c * P:(c + 1) * P], m.ident)
            last.then_inc(w_turned, 1)
            pe.wait_ge(w_ready, 1)
            for T in tiles:
                pe.wait_ge(quanted, T // 4 + 1)
                for c in range(C):
                    last = nc.tensor.matmul(bank(4 + T // 2, 256 * (T % 2), 256 * (T % 2) + 256),
                                            quant[:, c, P * T:P * T + P], wT[:, c, :],
                                            start=(c == 0), stop=(c == C - 1))
                if T % 2:
                    last.then_inc(multiplied, 1)

        @block.scalar
        def _(act):
            act.wait_ge(s_gamma, 16)
            for k in range(4):
                g, c = k // 2, k % 2
                act.wait_ge(ln["xT"], 4 * g + 4)
                nc.scalar.activation(full[:, c, 512 * g:512 * g + 512], bank(k), ACT.Copy,
                                     scale=gamma[:, c:c + 1]).then_inc(gained, 1)
            act.wait_ge(w_turned, 1)
            nc.scalar.activation(wT.rearrange("p c o -> p (c o)"), bank(4), ACT.Copy).then_inc(w_ready, 1)


def layer1_ctx_attention(nc, m):
    x, hT, sem, bank, psf = m.x, m.hT, m.sem, m.bank, m.psf
    tiles = list(range(NT))
    ln = m.ln_sems("x1")
    ps_kv = bank(6, 0, 384).rearrange("p (t d) -> p t d", t=3)
    q_rows = [bank(0, 0, 256), bank(4, 0, 256)]
    ps_pT = bank(3)
    ps_o = bank(7, 0, 256)
    kc = m.rope_a[:].rearrange("p a b c -> p (a b c)")
    tabk_cos = kc[:, 0:384].rearrange("p (t d) -> p t d", t=3)
    tabk_sin = kc[:, 384:768].rearrange("p (t d) -> p t d", t=3)
    norm_w = kc[:, 768:1024].rearrange("p (a d) -> p a d", a=2)
    kwork = m.xn[:].rearrange("p t d -> p (t d)")
    k_a = kwork[:, 0:384].rearrange("p (t d) -> p t d", t=3)
    k_b = kwork[:, 384:768].rearrange("p (t d) -> p t d", t=3)
    junk = [kwork[:, 768 + HD * i:768 + HD * i + HD] for i in range(5)]
    q_a = m.rope_b[:, 0]
    rq = m.small[:, 0:8].rearrange("p (j t) -> p j t", j=4)
    rk = m.small[:, 8:11]
    eps = m.small[:, 12:15]
    group_sum = m.qk_raw[:, 0].rearrange("p t d -> p (t d)")
    piece_full = kwork[:, 1664:1920]
    tabq_cos, tabq_sin = m.tab_cos[:, :, 0], m.tab_sin[:, :, 0]
    qa = [m.rope_b[:, p, 0].rearrange("p (t d) -> p t d", t=2) for p in range(2)]
    qb = [m.rope_b[:, p, 1].rearrange("p (t d) -> p t d", t=2) for p in range(2)]
    s_nw, s_tab, s_pre = sem("x1_nw"), sem("x1_tab"), sem("x1_pre")
    K = ("q", "sq", "rq0", "rq", "ra", "rb", "rope", "qT", "qhi", "qlo", "score", "max", "bias", "exp", "inv", "norm0", "norm1",
         "pT", "phi", "plo", "o", "ohi", "olo", "wo", "wo_out", "x",
         "k", "v", "ksq", "rk0", "rk", "ka", "kb", "krope", "vhi", "vlo", "kT", "khi", "klo",
         "load", "wfull", "whi", "wlo")
    s = {k: sem("x1_" + k) for k in K}
    N = B * G
    wf = {k: m.io["L1_ffn_" + k].rearrange("(c p) n -> p c n", p=P) for k in ("wq", "wk", "wv")}
    wf_o = m.io["L1_ffn_wo"].rearrange("(h p) d -> p h d", p=P)

    with nc.Block() as block:

        @block.sync
        def _(sp):
            for i, k in enumerate(("L1_xattn_q_norm_w", "L1_xattn_k_norm_w")):
                sp.dma_start(norm_w[:, i], m.io[k].partition_broadcast(P)).then_inc(s_nw, 16)
            def load(n):
                for i, k in enumerate(("wq", "wk", "wv")):
                    sp.dma_start(m.piece[:, i].rearrange("p (c d) -> p c d", c=C),
                                 wf[k][:, :, bass.ds(n * HD, HD)]).then_inc(s["load"], 16)
                sp.dma_start(m.piece[:, 3], wf_o[:, n]).then_inc(s["load"], 16)

            load(0)
            with sp.Fori(1, N) as n:
                sp.wait_ge(s["wlo"], 4 * n)
                load(n)

        @block.tensor
        def _(pe):
            def kv_project(n, part):
                b, g = n // G, n % G
                if part == 0:
                    done(pe, s["khi"], n)
                    done(pe, s["klo"], n)
                else:
                    pe.wait_ge(s["ka"], 3 * n + 3)
                    pe.wait_ge(s["kb"], 2 * n + 2)
                for t in range(3):
                    for c in range(C):
                        for i, (a, w) in enumerate(PASSES):
                            rows = m.ctxT[:, a, c, b, :] if t == 0 else hT[:, a, c, bass.ds(b * S + t * P - P, P)]
                            cols = m.w_xkv[:, w, c, int(t == 0), part, bass.ds(g * HD, HD)]
                            last = nc.tensor.matmul(ps_kv[:, t], rows, cols, start=(c == 0 and i == 0),
                                                    stop=(c == C - 1 and i == 2))
                last.then_inc(s["v" if part else "k"], 1)

            def k_turn(n):
                pe.wait_ge(s["krope"], n + 1)
                pe.wait_ge(s["vlo"], 3 * n + 3)
                for t in range(3):
                    last = nc.tensor.transpose(bank(6, P * t, P * t + P), k_a[:, t], m.ident)
                last.then_inc(s["kT"], 1)

            def q_project(n, j):
                b, h = n // G, (n % G) * G + j
                k = 4 * n + j
                done(pe, s["ra"], k - 1)
                done(pe, s["rb"], k - 1)
                for t in range(2):
                    for c in range(C):
                        for i, (a, w) in enumerate(PASSES):
                            last = nc.tensor.matmul(q_rows[j % 2][:, P * t:P * t + P],
                                                    hT[:, a, c, bass.ds(b * S + t * P, P)],
                                                    m.w_xq[:, w, c, bass.ds(h * HD, HD)],
                                                    start=(c == 0 and i == 0), stop=(c == C - 1 and i == 2))
                last.then_inc(s["q"], 1)

            def q_turn(n, j):
                k = 4 * n + j
                pe.wait_ge(s["rope"], k + 1)
                done(pe, s["qhi"], k)
                done(pe, s["qlo"], k)
                for t in range(2):
                    last = nc.tensor.transpose(bank(1, P * t, P * t + P), qa[j % 2][:, t], m.ident)
                last.then_inc(s["qT"], 1)

            def score(n, j):
                k = 4 * n + j
                pe.wait_ge(s["qlo"], k + 1)
                pe.wait_ge(s["qhi"], k + 1)
                if j == 0:
                    pe.wait_ge(s["klo"], n + 1)
                    pe.wait_ge(s["khi"], n + 1)
                done(pe, s["exp"], 2 * k)
                done(pe, s["max"], 2 * k)
                for t, diagonal, spans in ((0, 0, ((0, 64, 128), (128, 0, 64))), (1, 384, ((192, 0, 320),))):
                    nc.tensor.matmul(bank(2, diagonal, diagonal + P), m.ident_bf[:], m.causal_bf[:],
                                     start=True, stop=False, skip_group_check=True)
                    for i, (a, w) in enumerate(PASSES):
                        for at, k0, width in spans:
                            last = nc.tensor.matmul(bank(2, at, at + width), m.qkT[:, j % 2, a, P * t:P * t + P],
                                                    m.kT[:, n % 2, w, k0:k0 + width], start=False, stop=(i == 2),
                                                    skip_group_check=True)
                last.then_inc(s["score"], 1)

            def prob_turn(n, j):
                k = 4 * n + j
                pe.wait_ge(s["norm0"], k + 1)
                pe.wait_ge(s["norm1"], k + 1)
                done(pe, s["phi"], k)
                done(pe, s["plo"], k)
                pr = m.prob[:, j % 2]
                for at, src in ((0, 0), (128, 256), (256, 384), (384, 128)):
                    last = nc.tensor.transpose(ps_pT[:, at:at + P], pr[:, src:src + P], m.ident)
                last.then_inc(s["pT"], 1)

            def attend(n, j):
                k = 4 * n + j
                pe.wait_ge(s["plo"], k + 1)
                pe.wait_ge(s["phi"], k + 1)
                done(pe, s["ohi"], k)
                done(pe, s["olo"], k)
                for t, p0, o0, w_ in ((2, 0, 0, 256), (3, 256, 128, 128), (0, 384, 0, 128), (1, 384, 128, 128)):
                    for i, (a, w) in enumerate(PASSES):
                        last = nc.tensor.matmul(ps_o[:, o0:o0 + w_], m.vpair[:, n % 2, a, t],
                                                m.probT[:, j % 2, w, p0:p0 + w_], start=(t == 2 and i == 0),
                                                stop=(t == 1 and i == 2), skip_group_check=True)
                last.then_inc(s["o"], 1)

            def out_project(n, j):
                h, k = (n % G) * G + j, 4 * n + j
                pe.wait_ge(s["olo"], k + 1)
                pe.wait_ge(s["ohi"], k + 1)
                if j == 0:
                    done(pe, s["wo_out"], n)
                for t in range(2):
                    for i, (a, w) in enumerate(PASSES):
                        last = nc.tensor.matmul(bank(5, 256 * t, 256 * t + 256),
                                                m.oT[:, j % 2, a, P * t:P * t + P], m.w_xo[:, w, h],
                                                start=(j == 0 and i == 0 and t == 0), stop=(j == 3 and i == 2),
                                                skip_group_check=True)
                last.then_inc(s["wo"], 1)

            def slots(n, first, last):
                for j in range(4):
                    if not (last and j == 3):
                        score(n + (j + 1) // 4, (j + 1) % 4)
                    prob_turn(n, j)
                    if j == 0 and not last:
                        kv_project(n + 1, 0)
                    if not (last and j >= 2):
                        q_turn(n + (j + 2) // 4, (j + 2) % 4)
                    if not (first and j == 0):
                        out_project(n - (j == 0), (j - 1) % 4)
                    if j == 1 and not last:
                        kv_project(n + 1, 1)
                    if j == 2 and not last:
                        k_turn(n + 1)
                    if not last:
                        q_project(n + 1, j)
                    attend(n, j)

            m.ln_turn(pe, ln, tiles, 0)
            pe.wait_ge(ln["lo"], 4)
            kv_project(0, 0)
            q_project(0, 0)
            kv_project(0, 1)
            q_project(0, 1)
            q_turn(0, 0)
            k_turn(0)
            q_project(0, 2)
            q_turn(0, 1)
            score(0, 0)
            q_project(0, 3)
            slots(0, True, False)
            with pe.Fori(1, N - 1) as n:
                slots(n, False, False)
            slots(N - 1, False, True)
            out_project(N - 1, 3)

        @block.scalar
        def _(act):
            def k_squares(n):
                act.wait_ge(s["k"], n + 1)
                done(act, s["ka"], 3 * n)
                done(act, s["kb"], 2 * n)
                done(act, s["ksq"], n)
                for t in range(3):
                    last = nc.scalar.activation(junk[2 + t], ps_kv[:, t], ACT.Square, scale=MEAN_SQ,
                                                accum_out=rk[:, t:t + 1])
                last.then_inc(s["ksq"], 1)

            def v_hi(n):
                act.wait_ge(s["v"], n + 1)
                done(act, s["o"], 4 * n - 4)
                for i in range(2):
                    rows = slice(64 * i, 64 * i + 64)
                    nc.scalar.activation(m.vpair[rows, n % 2, 0, i], ps_kv[rows, 0], ACT.Copy,
                                         scale=1.0 / WS).then_inc(s["vhi"], 1)
                nc.scalar.activation(m.vpair[:, n % 2, 0, 2:4], ps_kv[:, 1:3], ACT.Copy,
                                     scale=1.0 / WS).then_inc(s["vhi"], 1)

            def k_hi(n):
                act.wait_ge(s["kT"], n + 1)
                done(act, s["score"], 4 * n - 4)
                nc.scalar.activation(m.kT[:, n % 2, 0], bank(6, 64, 384), ACT.Copy).then_inc(s["khi"], 1)

            def q_squares(n, j):
                k = 4 * n + j
                act.wait_ge(s["q"], k + 1)
                done(act, s["exp"], 2 * k - 6)
                done(act, s["bias"], k - 3)
                done(act, s["sq"], k)
                for t in range(2):
                    last = nc.scalar.activation(junk[t], q_rows[j % 2][:, P * t:P * t + P], ACT.Square,
                                                scale=MEAN_SQ, accum_out=rq[:, j, t:t + 1])
                last.then_inc(s["sq"], 1)

            def q_hi(n, j):
                k = 4 * n + j
                act.wait_ge(s["qT"], k + 1)
                done(act, s["score"], k - 1)
                nc.scalar.activation(m.qkT[:, j % 2, 0, 0:256], bank(1, 0, 256), ACT.Copy).then_inc(s["qhi"], 1)

            def exponent(n, j):
                k = 4 * n + j
                act.wait_ge(s["bias"], k + 1)
                done(act, s["pT"], k - 1)
                done(act, s["inv"], k - 1)
                for t, (a0, a1) in enumerate(((0, 192), (192, 512))):
                    nc.scalar.activation(m.prob[:, j % 2, a0:a1], bank(2, a0, a1), ACT.Exp,
                                         bias=m.exp_bias[:, j % 2, t:t + 1], scale=rq[:, j, t:t + 1],
                                         accum_out=m.row_sum[:, j % 2, t:t + 1]).then_inc(s["exp"], 1)

            def prob_norm(n, j):
                k = 4 * n + j
                act.wait_ge(s["inv"], k + 1)
                nc.scalar.activation(m.prob[:, j % 2, 0:192], m.prob[:, j % 2, 0:192], ACT.Copy,
                                     scale=m.inv_sum[:, j % 2, 0:1]).then_inc(s["norm0"], 1)

            def prob_hi(n, j):
                k = 4 * n + j
                act.wait_ge(s["pT"], k + 1)
                done(act, s["o"], k - 1)
                nc.scalar.activation(m.probT[:, j % 2, 0], ps_pT, ACT.Copy).then_inc(s["phi"], 1)

            def piece_hi(n, j):
                if j == 0:
                    act.wait_ge(s["load"], 64 * (n + 1))
                if j < 3:
                    w, hi = m.piece[:, j].rearrange("p (c d) -> p c d", c=C), m.w_fqkv[:, 0, :, j, bass.ds(n * HD, HD)]
                else:
                    w, hi = m.piece[:, 3], m.w_fo[:, 0, n]
                nc.scalar.activation(hi, w, ACT.Copy, scale=WS).then_inc(s["whi"], 1)

            def out_hi(n, j):
                k = 4 * n + j
                act.wait_ge(s["o"], k + 1)
                done(act, s["wo"], k - 1)
                nc.scalar.activation(m.oT[:, j % 2, 0], ps_o, ACT.Copy).then_inc(s["ohi"], 1)

            def group_out(n):
                act.wait_ge(s["wo"], 4 * n + 4)
                act.wait_ge(s["x"], n + 1)
                nc.scalar.activation(group_sum, bank(5), ACT.Copy, scale=1.0 / WS).then_inc(s["wo_out"], 1)

            def slots(n, first, last):
                for j in range(4):
                    prob_hi(n, j)
                    if j != 0 and not (last and j >= 2):
                        q_hi(n + (j + 2) // 4, (j + 2) % 4)
                    if j == 2 and not last:
                        k_hi(n + 1)
                    if not (last and j == 3):
                        exponent(n + (j + 1) // 4, (j + 1) % 4)
                    if j == 0:
                        q_hi(n, 2)
                    if j == 0 and not last:
                        k_squares(n + 1)
                    if j == 1 and not last:
                        v_hi(n + 1)
                    if not (last and j == 3):
                        prob_norm(n + (j + 1) // 4, (j + 1) % 4)
                    out_hi(n, j)
                    if not last:
                        q_squares(n + 1, j)
                    if j == 0 and not first:
                        group_out(n - 1)
                    piece_hi(n, j)

            m.ln_hi(act, ln, 0, 2)
            nc.scalar.preload_act_table(ACT.Exp)
            k_squares(0)
            q_squares(0, 0)
            v_hi(0)
            q_squares(0, 1)
            q_hi(0, 0)
            k_hi(0)
            q_squares(0, 2)
            q_hi(0, 1)
            exponent(0, 0)
            prob_norm(0, 0)
            q_squares(0, 3)
            slots(0, True, False)
            with act.Fori(1, N - 1) as n:
                slots(n, False, False)
            slots(N - 1, False, True)
            group_out(N - 1)

        @block.vector
        def _(dve):
            def v_lo(n):
                dve.wait_ge(s["vhi"], 3 * n + 3)
                for i in range(2):
                    rows = slice(64 * i, 64 * i + 64)
                    nc.vector.scalar_tensor_tensor(out=m.vpair[rows, n % 2, 1, i], in0=ps_kv[rows, 0],
                                                   scalar=1.0 / WS, in1=m.vpair[rows, n % 2, 0, i], op0=ALU.mult,
                                                   op1=ALU.subtract).then_inc(s["vlo"], 1)
                nc.vector.scalar_tensor_tensor(out=m.vpair[:, n % 2, 1, 2:4], in0=ps_kv[:, 1:3],
                                               scalar=1.0 / WS, in1=m.vpair[:, n % 2, 0, 2:4], op0=ALU.mult,
                                               op1=ALU.subtract).then_inc(s["vlo"], 1)

            def k_rows(n):
                dve.wait_ge(s["rk"], n + 1)
                done(dve, s["kT"], n)
                done(dve, s["krope"], n)
                for t in range(3):
                    nc.vector.scalar_tensor_tensor(out=k_a[:, t], in0=ps_kv[:, t], scalar=rk[:, t:t + 1],
                                                   in1=tabk_cos[:, t], op0=ALU.mult, op1=ALU.mult).then_inc(s["ka"], 1)
                for t in (1, 2):
                    src = ps_kv[:, t].rearrange("p (a d) -> p a d", a=2)[:, ::-1, :]
                    nc.vector.scalar_tensor_tensor(out=k_b[:, t].rearrange("p (a d) -> p a d", a=2), in0=src,
                                                   scalar=rk[:, t:t + 1],
                                                   in1=tabk_sin[:, t].rearrange("p (a d) -> p a d", a=2),
                                                   op0=ALU.mult, op1=ALU.mult).then_inc(s["kb"], 1)

            def k_lo(n):
                dve.wait_ge(s["khi"], n + 1)
                nc.vector.tensor_tensor(m.kT[:, n % 2, 1], bank(6, 64, 384), m.kT[:, n % 2, 0],
                                        ALU.subtract).then_inc(s["klo"], 1)

            def q_rope(n, j):
                k = 4 * n + j
                rows = q_rows[j % 2].rearrange("p (t d) -> p t d", t=2)
                dve.wait_ge(s["sq"], k + 1)
                done(dve, s["qT"], k - 1)
                done(dve, s["rope"], k - 1)
                nc.vector.tensor_tensor(qa[j % 2], rows, tabq_cos, ALU.mult).then_inc(s["ra"], 1)
                nc.vector.tensor_tensor(halves(qb[j % 2]), swap_halves(rows), halves(tabq_sin), ALU.mult).then_inc(s["rb"], 1)

            def q_lo(n, j):
                k = 4 * n + j
                dve.wait_ge(s["qhi"], k + 1)
                nc.vector.tensor_tensor(m.qkT[:, j % 2, 1, 0:256], bank(1, 0, 256), m.qkT[:, j % 2, 0, 0:256],
                                        ALU.subtract).then_inc(s["qlo"], 1)

            def row_max(n, j):
                k = 4 * n + j
                dve.wait_ge(s["score"], k + 1)
                for t, (a0, a1) in enumerate(((0, 192), (192, 512))):
                    nc.vector.tensor_reduce(m.neg_max[:, j % 2, t:t + 1], bank(2, a0, a1), AX.X, ALU.max,
                                            negate=True).then_inc(s["max"], 1)
                dve.wait_ge(s["max"], 2 * k + 2)
                dve.wait_ge(s["rq"], k + 1)
                nc.vector.tensor_tensor(m.exp_bias[:, j % 2], m.neg_max[:, j % 2], rq[:, j], ALU.mult).then_inc(s["bias"], 1)

            def row_inv(n, j):
                k = 4 * n + j
                dve.wait_ge(s["exp"], 2 * k + 2)
                done(dve, s["norm0"], k - 1)
                done(dve, s["norm1"], k - 1)
                nc.vector.reciprocal(m.inv_sum[:, j % 2], m.row_sum[:, j % 2]).then_inc(s["inv"], 1)
                dve.wait_ge(s["inv"], k + 1)
                nc.vector.tensor_scalar(m.prob[:, j % 2, 192:512], m.prob[:, j % 2, 192:512],
                                        m.inv_sum[:, j % 2, 1:2], None, ALU.mult).then_inc(s["norm1"], 1)

            def prob_lo(n, j):
                k = 4 * n + j
                dve.wait_ge(s["phi"], k + 1)
                nc.vector.tensor_tensor(m.probT[:, j % 2, 1], ps_pT, m.probT[:, j % 2, 0],
                                        ALU.subtract).then_inc(s["plo"], 1)

            def out_lo(n, j):
                k = 4 * n + j
                dve.wait_ge(s["ohi"], k + 1)
                nc.vector.tensor_tensor(m.oT[:, j % 2, 1], ps_o, m.oT[:, j % 2, 0],
                                        ALU.subtract).then_inc(s["olo"], 1)

            def slots(n, first, last):
                for j in range(4):
                    if not (last and j == 3):
                        row_max(n + (j + 1) // 4, (j + 1) % 4)
                    prob_lo(n, j)
                    if not (last and j >= 2):
                        q_lo(n + (j + 2) // 4, (j + 2) % 4)
                    if j == 2 and not last:
                        k_lo(n + 1)
                    if not (last and j >= 1):
                        q_rope(n + (j + 3) // 4, (j + 3) % 4)
                    if not (last and j == 3):
                        row_inv(n + (j + 1) // 4, (j + 1) % 4)
                    out_lo(n, j)
                    if j == 0 and not last:
                        k_rows(n + 1)
                    if j == 1 and not last:
                        v_lo(n + 1)

            m.ln_stats(dve, ln, tiles)
            dve.wait_ge(s_nw, 32)
            cos = m.cst("cos").rearrange("p (t d) -> p t d", t=2)
            sin = m.cst("sin").rearrange("p (t d) -> p t d", t=2)
            for dst, w, tab, f in ((tabq_cos, 0, cos, HD ** -0.5), (tabk_cos[:, 1:3], 1, cos, 1.0)):
                gain = norm_w[:, w].unsqueeze(1).broadcast_to([P, 2, HD])
                nc.vector.scalar_tensor_tensor(out=dst, in0=gain, scalar=f / WS, in1=tab,
                                               op0=ALU.mult, op1=ALU.mult).then_inc(s_tab, 1)
            for dst, w, f in ((tabq_sin, 0, HD ** -0.5), (tabk_sin[:, 1:3], 1, 1.0)):
                for t in range(2):
                    gain = norm_w[:, w].rearrange("p (a d) -> p a d", a=2)[:, ::-1, :]
                    nc.vector.scalar_tensor_tensor(out=dst[:, t].rearrange("p (a d) -> p a d", a=2), in0=gain,
                                                   scalar=f / WS, in1=sin[:, t].rearrange("p (a d) -> p a d", a=2),
                                                   op0=ALU.mult, op1=ALU.mult).then_inc(s_tab, 1)
            nc.vector.tensor_scalar(tabk_cos[:, 0], norm_w[:, 1], 1.0 / WS, None, ALU.mult).then_inc(s_tab, 1)
            dve.wait_ge(s_tab, 7)
            m.ln_apply(dve, ln, tiles)
            m.ln_lo(dve, ln, 0, 2)
            k_rows(0)
            q_rope(0, 0)
            v_lo(0)
            q_rope(0, 1)
            q_lo(0, 0)
            k_lo(0)
            q_rope(0, 2)
            q_lo(0, 1)
            row_max(0, 0)
            row_inv(0, 0)
            slots(0, True, False)
            with dve.Fori(1, N - 1) as n:
                slots(n, False, False)
            slots(N - 1, False, True)

        @block.gpsimd
        def _(pool):
            def k_inv(n):
                pool.wait_ge(s["ksq"], n + 1)
                nc.gpsimd.tensor_tensor(rk, rk, eps, ALU.add).then_inc(s["rk0"], 1)
                pool.wait_ge(s["rk0"], n + 1)
                nc.gpsimd.tensor_tensor(rk, rk, m.neg_half[:, 0:3], ALU.pow).then_inc(s["rk"], 1)

            def q_inv(n, j):
                k = 4 * n + j
                pool.wait_ge(s["sq"], k + 1)
                nc.gpsimd.tensor_tensor(rq[:, j], rq[:, j], eps[:, 0:2], ALU.add).then_inc(s["rq0"], 1)
                pool.wait_ge(s["rq0"], k + 1)
                nc.gpsimd.tensor_tensor(rq[:, j], rq[:, j], m.neg_half[:, 0:2], ALU.pow).then_inc(s["rq"], 1)

            def k_sum(n):
                pool.wait_ge(s["ka"], 3 * n + 3)
                pool.wait_ge(s["kb"], 2 * n + 2)
                nc.gpsimd.tensor_tensor(k_a[:, 1:3], k_a[:, 1:3], k_b[:, 1:3], ALU.add).then_inc(s["krope"], 1)

            def rope_sum(n, j):
                k = 4 * n + j
                pool.wait_ge(s["ra"], k + 1)
                pool.wait_ge(s["rb"], k + 1)
                nc.gpsimd.tensor_tensor(qa[j % 2], qa[j % 2], qb[j % 2], ALU.add).then_inc(s["rope"], 1)

            def residual(n):
                pool.wait_ge(s["wo_out"], n + 1)
                pool.wait_ge(s["x"], n + 1)
                rows = x[:, bass.ds(n // G * 2, 2), :].rearrange("p t d -> p (t d)")
                nc.gpsimd.tensor_tensor(rows, rows, group_sum, ALU.add).then_inc(s["x"], 1)

            def split_piece(n, j):
                k = 4 * n + j
                if j == 0:
                    pool.wait_ge(s["load"], 64 * (n + 1))
                if j < 3:
                    by_chunk = "p (c d) -> p c d"
                    w, full = (ap.rearrange(by_chunk, c=C) for ap in (m.piece[:, j], piece_full))
                    scale = m.ws_row[:].rearrange(by_chunk, c=C)
                    hi, lo = (m.w_fqkv[:, hl, :, j, bass.ds(n * HD, HD)] for hl in range(2))
                else:
                    w, full, scale = m.piece[:, 3], piece_full, m.ws_row[:]
                    hi, lo = (m.w_fo[:, hl, n] for hl in range(2))
                done(pool, s["wlo"], k)
                nc.gpsimd.tensor_tensor(full, w, scale, ALU.mult).then_inc(s["wfull"], 1)
                pool.wait_ge(s["wfull"], k + 1)
                pool.wait_ge(s["whi"], k + 1)
                nc.gpsimd.tensor_tensor(lo, full, hi, ALU.subtract).then_inc(s["wlo"], 1)

            def slots(n, first, last):
                for j in range(4):
                    if j == 1 and not last:
                        k_sum(n + 1)
                    if j == 0 and not last:
                        k_inv(n + 1)
                    if not (last and j >= 1):
                        rope_sum(n + (j + 3) // 4, (j + 3) % 4)
                    if not (last and j >= 1):
                        q_inv(n + (j + 3) // 4, (j + 3) % 4)
                    if j == 1 and not first:
                        residual(n - 1)
                    split_piece(n, j)

            m.ln_rstd(pool, ln, tiles)
            nc.gpsimd.memset(eps, 1e-6).then_inc(s_pre, 1)
            pool.sem_inc(s["x"], 1)
            pool.wait_ge(s_pre, 1)
            k_inv(0)
            k_sum(0)
            q_inv(0, 0)
            rope_sum(0, 0)
            q_inv(0, 1)
            rope_sum(0, 1)
            q_inv(0, 2)
            rope_sum(0, 2)
            slots(0, True, False)
            with pool.Fori(1, N - 1) as n:
                slots(n, False, False)
            slots(N - 1, False, True)
            residual(N - 1)


def layer1_attention(nc, m):
    x, h_, hT, sem, bank = m.x, m.h, m.hT, m.sem, m.bank
    row_scale = m.small[:, 16:24]
    tiles = list(range(NT))
    ln = m.ln_sems("f1")
    bias = m.w_xkv[:].rearrange("p a c s k n -> p (a c s k n)").bitcast(F32).rearrange(
        "p (h k d) -> p h k d", h=H, k=2)
    out_bias = m.xn[:].rearrange("p t d -> p (t d)")[:, 0:256]
    v = m.vpair[:].rearrange("p a b c d -> p (a b c d)")
    qk_raw = [m.qk_raw[:, p] for p in range(2)]
    vbuf = [v[:, 512 * i:512 * i + 512].rearrange("p (a t d) -> p a t d", a=2, t=2) for i in range(4)]
    group_sum = m.xn[:].rearrange("p t d -> p (t d)")[:, 512:1024]
    piece_full = m.xn[:].rearrange("p t d -> p (t d)")[:, 256:384]
    ln_gain, ln_shift, v_bias = m.fcols[:, 2:4], m.fcols[:, 4:6], m.fcols[:, 6:22]
    xn, s_h, s_var_h, s_scale = m.xn, sem("f1_h"), sem("f1_var_h"), sem("f1_scale")
    s_vec, s_bias, s_ob, s_ready = sem("f1_vec"), sem("f1_bias"), sem("f1_ob"), sem("f1_ready")
    K = ("qkv", "raw", "ra", "rb", "rope", "qT", "qhi", "qlo", "score", "max", "exp", "inv", "norm0", "norm1",
         "pT", "phi", "plo", "o", "ohi", "olo", "wo", "wo_out", "x", "vhi", "vlo", "load", "wfull", "whi", "wlo")
    s = {k: sem("f1_" + k) for k in K}
    N = B * G
    up = m.io["L1_ffn_we1"].rearrange("e (c p) i -> p (e c) i", p=P)
    down = m.io["L1_ffn_we2"].rearrange("e (c p) d -> p (e c) d", p=P)

    def heads(n):
        return (n % G) * G

    with nc.Block() as block:

        @block.sync
        def _(sp):
            with nc.allow_non_contiguous_dma(reason="feature vectors, one number per partition"):
                for dst, k in ((ln_gain, "ln1_w"), (ln_shift, "ln1_b"), (v_bias, "bv")):
                    sp.dma_start(dst, m.io["L1_ffn_" + k].rearrange("(c p) -> p c", p=P)).then_inc(s_vec, 16)
            for i, k in enumerate(("bq", "bk")):
                sp.dma_start(bias[:, :, i], m.io["L1_ffn_" + k].partition_broadcast(P).rearrange(
                    "p (h d) -> p h d", d=HD)).then_inc(s_bias, 16)
            sp.wait_ge(ln["lo"], 4)
            sp.dma_start(out_bias, m.io["L1_ffn_bo"].partition_broadcast(P)).then_inc(s_ob, 16)
            def load(n):
                for i, w in enumerate((up, down)):
                    sp.dma_start(m.piece[:, i, 0:P], w[:, n // 2, bass.ds((n % 2) * P, P)]).then_inc(s["load"], 16)

            load(0)
            with sp.Fori(1, N) as n:
                sp.wait_ge(s["wlo"], 2 * n)
                load(n)

        @block.tensor
        def _(pe):
            def project(n, j):
                b, h, k = n // G, heads(n) + j, 4 * n + j
                done(pe, s["raw"], k - 1)
                done(pe, s["vlo"], k)
                for t in range(2):
                    for c in range(C):
                        for i, (a, w) in enumerate(PASSES):
                            rows = hT[:, a, c, bass.ds(b * S + t * P, P)]
                            nc.tensor.matmul(bank(j % 2, 256 * t, 256 * t + 256), rows,
                                             m.w_fqkv[:, w, c, 0:2, bass.ds(h * HD, HD)],
                                             start=(c == 0 and i == 0), stop=(c == C - 1 and i == 2))
                            last = nc.tensor.matmul(bank(2, P * t, P * t + P), rows,
                                                    m.w_fqkv[:, w, c, 2, bass.ds(h * HD, HD)],
                                                    start=(c == 0 and i == 0), stop=(c == C - 1 and i == 2))
                last.then_inc(s["qkv"], 1)

            def turn(n, j):
                k = 4 * n + j
                pe.wait_ge(s["rope"], k + 1)
                done(pe, s["qhi"], k)
                done(pe, s["qlo"], k)
                for i in range(2):
                    for t in range(2):
                        at = 256 * i + P * t
                        last = nc.tensor.transpose(bank(3, at, at + P), m.rope_a[:, j % 2, t, P * i:P * i + P], m.ident)
                last.then_inc(s["qT"], 1)

            def score(n, j):
                k = 4 * n + j
                pe.wait_ge(s["qlo"], k + 1)
                pe.wait_ge(s["qhi"], k + 1)
                done(pe, s["exp"], 2 * k)
                done(pe, s["max"], 2 * k)
                for t, (a0, a1) in enumerate(((0, 128), (128, 384))):
                    nc.tensor.matmul(bank(4, a1 - P, a1), m.ident_bf[:], m.causal_bf[:],
                                     start=True, stop=False, skip_group_check=True)
                    for i, (a, w) in enumerate(PASSES):
                        last = nc.tensor.matmul(bank(4, a0, a1), m.qkT[:, j % 2, a, P * t:P * t + P],
                                                m.qkT[:, j % 2, w, 256:256 + a1 - a0], start=False, stop=(i == 2),
                                                skip_group_check=True)
                last.then_inc(s["score"], 1)

            def prob_turn(n, j):
                k = 4 * n + j
                pe.wait_ge(s["norm0"], k + 1)
                pe.wait_ge(s["norm1"], k + 1)
                done(pe, s["phi"], k)
                done(pe, s["plo"], k)
                for at in (0, 128, 256):
                    last = nc.tensor.transpose(bank(5, at, at + P), m.prob[:, j % 2, at:at + P], m.ident)
                last.then_inc(s["pT"], 1)

            def attend(n, j):
                k = 4 * n + j
                pe.wait_ge(s["plo"], k + 1)
                pe.wait_ge(s["phi"], k + 1)
                done(pe, s["ohi"], k)
                done(pe, s["olo"], k)
                first = True
                for t, (p0, o0, w_) in enumerate(((0, 0, 256), (256, 128, 128))):
                    for i, (a, w) in enumerate(PASSES):
                        last = nc.tensor.matmul(bank(7, o0, o0 + w_), vbuf[j][:, a, t],
                                                m.probT[:, j % 2, w, p0:p0 + w_], start=first,
                                                stop=(t == 1 and i == 2), skip_group_check=True)
                        first = False
                last.then_inc(s["o"], 1)

            def out_project(n, j):
                h, k = heads(n) + j, 4 * n + j
                pe.wait_ge(s["olo"], k + 1)
                pe.wait_ge(s["ohi"], k + 1)
                if j == 0:
                    done(pe, s["wo_out"], n)
                for t in range(2):
                    for i, (a, w) in enumerate(PASSES):
                        last = nc.tensor.matmul(bank(6, 256 * t, 256 * t + 256),
                                                m.oT[:, j % 2, a, P * t:P * t + P], m.w_fo[:, w, h],
                                                start=(j == 0 and i == 0 and t == 0), stop=(j == 3 and i == 2),
                                                skip_group_check=True)
                last.then_inc(s["wo"], 1)

            def slots(n, first, last):
                for j in range(4):
                    prob_turn(n, j)
                    if not (last and j == 3):
                        score(n + (j + 1) // 4, (j + 1) % 4)
                    if not (last and j >= 2):
                        turn(n + (j + 2) // 4, (j + 2) % 4)
                    if not (first and j == 0):
                        out_project(n - (j == 0), (j - 1) % 4)
                    attend(n, j)
                    if not last:
                        project(n + 1, j)

            m.ln_turn(pe, ln, tiles, 0)
            pe.wait_ge(ln["lo"], 4)
            project(0, 0)
            project(0, 1)
            turn(0, 0)
            project(0, 2)
            turn(0, 1)
            score(0, 0)
            project(0, 3)
            slots(0, True, False)
            with pe.Fori(1, N - 1) as n:
                slots(n, False, False)
            slots(N - 1, False, True)
            out_project(N - 1, 3)

        @block.scalar
        def _(act):
            def v_hi(n, j):
                k = 4 * n + j
                act.wait_ge(s["qkv"], k + 1)
                done(act, s["o"], k - 3)
                src = bank(2, 0, 256).rearrange("p (t d) -> p t d", t=2)
                nc.scalar.activation(vbuf[j][:, 0], src, ACT.Copy, scale=1.0 / WS).then_inc(s["vhi"], 1)

            def qk_hi(n, j):
                k = 4 * n + j
                act.wait_ge(s["qT"], k + 1)
                done(act, s["score"], k - 1)
                nc.scalar.activation(m.qkT[:, j % 2, 0], bank(3), ACT.Copy).then_inc(s["qhi"], 1)

            def exponent(n, j):
                k = 4 * n + j
                act.wait_ge(s["max"], 2 * k + 2)
                done(act, s["pT"], k - 1)
                done(act, s["inv"], k - 1)
                for t, (a0, a1) in enumerate(((0, 128), (128, 384))):
                    nc.scalar.activation(m.prob[:, j % 2, a0:a1], bank(4, a0, a1), ACT.Exp,
                                         bias=m.neg_max[:, j % 2, t:t + 1],
                                         accum_out=m.row_sum[:, j % 2, t:t + 1]).then_inc(s["exp"], 1)

            def prob_norm(n, j):
                k = 4 * n + j
                act.wait_ge(s["inv"], k + 1)
                nc.scalar.activation(m.prob[:, j % 2, 0:P], m.prob[:, j % 2, 0:P], ACT.Copy,
                                     scale=m.inv_sum[:, j % 2, 0:1]).then_inc(s["norm0"], 1)

            def prob_hi(n, j):
                k = 4 * n + j
                act.wait_ge(s["pT"], k + 1)
                done(act, s["o"], k - 1)
                nc.scalar.activation(m.probT[:, j % 2, 0, 0:384], bank(5, 0, 384), ACT.Copy).then_inc(s["phi"], 1)

            def out_hi(n, j):
                k = 4 * n + j
                act.wait_ge(s["o"], k + 1)
                done(act, s["wo"], k - 1)
                nc.scalar.activation(m.oT[:, j % 2, 0], bank(7, 0, 256), ACT.Identity,
                                     bias=v_bias[:, bass.ds(heads(n) + j, 1)]).then_inc(s["ohi"], 1)

            def group_out(n):
                act.wait_ge(s["wo"], 4 * n + 4)
                act.wait_ge(s["x"], n + 1)
                nc.scalar.activation(group_sum, bank(6), ACT.Copy, scale=1.0 / WS).then_inc(s["wo_out"], 1)

            def slots(n, first, last):
                for j in range(4):
                    if not (last and j >= 1):
                        v_hi(n + (j + 3) // 4, (j + 3) % 4)
                    prob_hi(n, j)
                    if not (last and j >= 2):
                        qk_hi(n + (j + 2) // 4, (j + 2) % 4)
                    if not (last and j == 3):
                        exponent(n + (j + 1) // 4, (j + 1) % 4)
                    out_hi(n, j)
                    if not (last and j == 3):
                        prob_norm(n + (j + 1) // 4, (j + 1) % 4)
                    if j == 0 and not first:
                        group_out(n - 1)

            act.wait_ge(s_vec, 48)
            m.ln_hi(act, ln, 0, 2, ln_gain, ln_shift)
            nc.scalar.preload_act_table(ACT.Exp)
            v_hi(0, 0)
            v_hi(0, 1)
            qk_hi(0, 0)
            v_hi(0, 2)
            qk_hi(0, 1)
            exponent(0, 0)
            prob_norm(0, 0)
            slots(0, True, False)
            with act.Fori(1, N - 1) as n:
                slots(n, False, False)
            slots(N - 1, False, True)
            group_out(N - 1)

        @block.vector
        def _(dve):
            def raw(n, j):
                k = 4 * n + j
                dve.wait_ge(s["qkv"], k + 1)
                done(dve, s["ra"], k - 1)
                done(dve, s["rb"], k - 1)
                rows = bank(j % 2).rearrange("p (t n) -> p t n", t=2)
                add = bias[:, heads(n) + j].rearrange("p k d -> p (k d)").unsqueeze(1).broadcast_to([P, 2, 256])
                nc.vector.scalar_tensor_tensor(out=qk_raw[j % 2], in0=add, scalar=WS, in1=rows, op0=ALU.mult,
                                               op1=ALU.add).then_inc(s["raw"], 1)

            def v_lo(n, j):
                k = 4 * n + j
                dve.wait_ge(s["vhi"], k + 1)
                src = bank(2, 0, 256).rearrange("p (t d) -> p t d", t=2)
                nc.vector.scalar_tensor_tensor(out=vbuf[j][:, 1], in0=src, scalar=1.0 / WS, in1=vbuf[j][:, 0],
                                               op0=ALU.mult, op1=ALU.subtract).then_inc(s["vlo"], 1)

            def rope_sin(n, j):
                k = 4 * n + j
                dve.wait_ge(s["raw"], k + 1)
                done(dve, s["rope"], k - 1)

                def by_half(ap):
                    return ap.rearrange("p t (k a d) -> p (t k) a d", k=2, a=2)
                nc.vector.tensor_tensor(by_half(m.rope_b[:, j % 2]), by_half(qk_raw[j % 2])[:, :, ::-1, :],
                                        m.tab_sin[:].rearrange("p t k (a d) -> p (t k) a d", a=2),
                                        ALU.mult).then_inc(s["rb"], 1)

            def qk_lo(n, j):
                k = 4 * n + j
                dve.wait_ge(s["qhi"], k + 1)
                nc.vector.tensor_tensor(m.qkT[:, j % 2, 1], bank(3), m.qkT[:, j % 2, 0],
                                        ALU.subtract).then_inc(s["qlo"], 1)

            def row_max(n, j):
                k = 4 * n + j
                dve.wait_ge(s["score"], k + 1)
                done(dve, s["exp"], 2 * k - 2)
                for t, (a0, a1) in enumerate(((0, 128), (128, 384))):
                    nc.vector.tensor_reduce(m.neg_max[:, j % 2, t:t + 1], bank(4, a0, a1), AX.X, ALU.max,
                                            negate=True).then_inc(s["max"], 1)

            def row_inv(n, j):
                k = 4 * n + j
                dve.wait_ge(s["exp"], 2 * k + 2)
                done(dve, s["norm0"], k - 1)
                done(dve, s["norm1"], k - 1)
                nc.vector.reciprocal(m.inv_sum[:, j % 2], m.row_sum[:, j % 2]).then_inc(s["inv"], 1)
                dve.wait_ge(s["inv"], k + 1)
                nc.vector.tensor_scalar(m.prob[:, j % 2, P:3 * P], m.prob[:, j % 2, P:3 * P],
                                        m.inv_sum[:, j % 2, 1:2], None, ALU.mult).then_inc(s["norm1"], 1)

            def prob_lo(n, j):
                k = 4 * n + j
                dve.wait_ge(s["phi"], k + 1)
                nc.vector.tensor_tensor(m.probT[:, j % 2, 1, 0:384], bank(5, 0, 384), m.probT[:, j % 2, 0, 0:384],
                                        ALU.subtract).then_inc(s["plo"], 1)

            def out_lo(n, j):
                k = 4 * n + j
                dve.wait_ge(s["ohi"], k + 1)
                nc.vector.scalar_tensor_tensor(out=m.oT[:, j % 2, 1], in0=bank(7, 0, 256),
                                               scalar=v_bias[:, bass.ds(heads(n) + j, 1)], in1=m.oT[:, j % 2, 0],
                                               op0=ALU.add, op1=ALU.subtract).then_inc(s["olo"], 1)

            def slots(n, first, last):
                for j in range(4):
                    if not (last and j >= 1):
                        raw(n + (j + 3) // 4, (j + 3) % 4)
                    if not (last and j >= 1):
                        v_lo(n + (j + 3) // 4, (j + 3) % 4)
                    prob_lo(n, j)
                    if not (last and j == 3):
                        row_max(n + (j + 1) // 4, (j + 1) % 4)
                    if not (last and j >= 2):
                        qk_lo(n + (j + 2) // 4, (j + 2) % 4)
                    if not (last and j >= 1):
                        rope_sin(n + (j + 3) // 4, (j + 3) % 4)
                    if not (last and j == 3):
                        row_inv(n + (j + 1) // 4, (j + 1) % 4)
                    out_lo(n, j)

            m.ln_stats(dve, ln, tiles)
            for g in range(2):
                cols = slice(4 * g, 4 * g + 4)
                dve.wait_ge(ln["var"], 4 * g + 4)
                nc.vector.tensor_scalar(row_scale[:, cols], m.meanvar[:, cols, 1], 1.0 + 1e-5, 1e-10,
                                        ALU.mult, ALU.add).then_inc(s_var_h, 1)
            for i, f in enumerate((HD ** -0.5 / WS, 1.0 / WS)):
                for dst, src in ((m.tab_cos, "cos"), (m.tab_sin, "sin")):
                    nc.vector.tensor_scalar(dst[:, :, i], m.cst(src).rearrange("p (t d) -> p t d", t=2), f, None,
                                            ALU.mult).then_inc(s_ready, 1)
            for g in range(2):
                dve.wait_ge(s_scale, g + 1)
                for T in range(4 * g, 4 * g + 4):
                    nc.vector.tensor_scalar(xn[:, T, :], x[:, T, :], m.meanvar[:, T, 0:1], row_scale[:, T:T + 1],
                                            ALU.subtract, ALU.mult).then_inc(ln["xn"], 1)
            dve.wait_ge(s_vec, 48)
            m.ln_lo(dve, ln, 0, 2, ln_gain, ln_shift)
            dve.wait_ge(ln["rstd"], 2)
            for T in tiles:
                nc.vector.tensor_scalar(h_[:, T, :], x[:, T, :], m.meanvar[:, T, 0:1], m.rstd[:, T:T + 1],
                                        ALU.subtract, ALU.mult).then_inc(s_h, 1)
            dve.wait_ge(s_bias, 32)
            raw(0, 0)
            v_lo(0, 0)
            rope_sin(0, 0)
            raw(0, 1)
            v_lo(0, 1)
            rope_sin(0, 1)
            qk_lo(0, 0)
            raw(0, 2)
            v_lo(0, 2)
            rope_sin(0, 2)
            qk_lo(0, 1)
            row_max(0, 0)
            row_inv(0, 0)
            slots(0, True, False)
            with dve.Fori(1, N - 1) as n:
                slots(n, False, False)
            slots(N - 1, False, True)

        @block.gpsimd
        def _(pool):
            def rope_cos(n, j):
                k = 4 * n + j
                pool.wait_ge(s["raw"], k + 1)
                done(pool, s["qT"], k - 1)
                nc.gpsimd.tensor_tensor(m.rope_a[:, j % 2], qk_raw[j % 2],
                                        m.tab_cos[:].rearrange("p t k d -> p t (k d)"), ALU.mult).then_inc(s["ra"], 1)

            def rope_sum(n, j):
                k = 4 * n + j
                pool.wait_ge(s["ra"], k + 1)
                pool.wait_ge(s["rb"], k + 1)
                nc.gpsimd.tensor_tensor(m.rope_a[:, j % 2], m.rope_a[:, j % 2], m.rope_b[:, j % 2],
                                        ALU.add).then_inc(s["rope"], 1)

            def residual(n):
                pool.wait_ge(s["wo_out"], n + 1)
                pool.wait_ge(s["x"], n + 1)
                rows = h_[:, bass.ds(n // G * 2, 2), :].rearrange("p t d -> p (t d)")
                nc.gpsimd.tensor_tensor(rows, rows, group_sum, ALU.add).then_inc(s["x"], 1)

            def split_piece(n, j):
                k = 2 * n + j
                if j == 0:
                    pool.wait_ge(s["load"], 32 * (n + 1))
                w, scale, full = m.piece[:, j, 0:P], m.ws_row[:, 0:P], piece_full
                hi, lo = (m.w_xq_moe[:, hl, bass.ds(2048 * j + n * P, P)] for hl in range(2))
                done(pool, s["wlo"], k)
                nc.gpsimd.tensor_tensor(full, w, scale, ALU.mult).then_inc(s["wfull"], 1)
                nc.gpsimd.tensor_tensor(hi, w, scale, ALU.mult).then_inc(s["whi"], 1)
                pool.wait_ge(s["wfull"], k + 1)
                pool.wait_ge(s["whi"], k + 1)
                nc.gpsimd.tensor_tensor(lo, full, hi, ALU.subtract).then_inc(s["wlo"], 1)

            def slots(n, first, last):
                for j in range(4):
                    if not (last and j >= 1):
                        rope_cos(n + (j + 3) // 4, (j + 3) % 4)
                    if j < 2:
                        split_piece(n, j)
                    if j == 2 and not first:
                        residual(n - 1)
                    if not (last and j >= 1):
                        rope_sum(n + (j + 3) // 4, (j + 3) % 4)

            for g in range(2):
                cols = slice(4 * g, 4 * g + 4)
                pool.wait_ge(s_var_h, g + 1)
                nc.gpsimd.tensor_tensor(row_scale[:, cols], row_scale[:, cols], m.neg_half[:, cols],
                                        ALU.pow).then_inc(s_scale, 1)
            m.ln_rstd(pool, ln, tiles)
            pool.wait_ge(s_h, NT)
            pool.wait_ge(s_ob, 16)
            nc.gpsimd.tensor_tensor(h_[:], h_[:], out_bias.unsqueeze(1).broadcast_to([P, NT, D]), ALU.add).then_inc(s["x"], 1)
            pool.wait_ge(s_ready, 4)
            for j in range(3):
                rope_cos(0, j)
                rope_sum(0, j)
            slots(0, True, False)
            with pool.Fori(1, N - 1) as n:
                slots(n, False, False)
            slots(N - 1, False, True)
            residual(N - 1)


def layer1_moe(nc, m):
    x, xn, hT, sem, bank, psf = m.x, m.xn, m.hT, m.sem, m.bank, m.psf
    tiles = list(range(NT))
    ln = m.ln_sems("m1")
    ln_gain, ln_shift, up_bias = m.fcols[:, 22:24], m.fcols[:, 24:26], m.fcols[:, 26:34]
    w_up = m.w_xq_moe[:, :, 0:2048].rearrange("p a (e c i) -> p a e c i", e=E, c=C)
    w_down = m.w_xq_moe[:, :, 2048:4096].rearrange("p a (e c d) -> p a e c d", e=E, c=C)
    gate32 = m.scratch32[:, 0:8]
    gate = m.scratch[:, 16:32].rearrange("p (a c e) -> p a c e", a=2, c=C)
    down_bias = m.scratch32[:, 16:1040].rearrange("p (e d) -> p e d", e=E)
    hid = [m.scratch32[:, 1040 + 1024 * p:2064 + 1024 * p].rearrange("p (c n) -> p c n", c=C) for p in range(2)]
    hid_pair = [m.scratch[:, 6400 + 2048 * p:8448 + 2048 * p].rearrange("p (a c n) -> p a c n", a=2, c=C)
                for p in range(2)]
    r = m.scratch32[:, 9240:9240 + 6 * 32].rearrange("p (k t e) -> p k t e", k=6, t=NT)
    logit, raw, rank, tmp, comb = (r[:, i] for i in range(5))
    tmax, tsum = m.small[:, 0:8], m.small[:, 8:16]
    s_vec, s_gate, gate_hi, gate_lo, gated = (sem("m1_" + k) for k in ("vec", "gate", "gate_hi", "gate_lo", "gated"))
    s_route, s_exp, s_ready, s_ranked = sem("m1_route"), sem("m1_exp"), sem("m1_ready"), sem("m1_ranked")
    upped, geled, hid_hi, hid_lo, downed, added, stored = (
        sem("m1_" + k) for k in ("up", "gelu", "hid_hi", "hid_lo", "down", "added", "stored"))

    def biased_rows(u, t):
        return 8 * u + t + 1

    def summed_rows(u, t):
        return 8 * u + 4 + t + 1

    with nc.Block() as block:

        @block.sync
        def _(sp):
            with nc.allow_non_contiguous_dma(reason="feature vectors, one number per partition"):
                for dst, k in ((ln_gain, "ln2_w"), (ln_shift, "ln2_b")):
                    sp.dma_start(dst, m.io["L1_ffn_" + k].rearrange("(c p) -> p c", p=P)).then_inc(s_vec, 16)
                sp.dma_start(up_bias.rearrange("p (e c) -> p e c", e=E),
                             m.io["L1_ffn_be1"].rearrange("e (c p) -> p e c", p=P)).then_inc(s_vec, 16)
                sp.dma_start(gate32.rearrange("p (c e) -> p c e", c=C),
                             m.io["L1_ffn_w_gate"].rearrange("(c p) e -> p c e", p=P)).then_inc(s_gate, 16)
            sp.dma_start(down_bias, m.io["L1_ffn_be2"].rearrange("e d -> (e d)").partition_broadcast(P).rearrange(
                "p (e d) -> p e d", e=E)).then_inc(s_vec, 16)
            for T in tiles:
                sp.wait_ge(added, summed_rows(T // 4 * E + E - 1, T % 4))
                sp.dma_start(m.out.rearrange("b (t p) d -> p (b t) d", p=P)[:, T], x[:, T]).then_inc(stored, 16)
            sp.wait_ge(stored, 16 * NT)

        @block.gpsimd
        def _(pool):
            m.ln_rstd(pool, ln, tiles)
            nc.gpsimd.tensor_tensor(x[:], x[:], m.h[:], ALU.add).then_inc(s_ready, 1)
            for u in range(2 * E):
                pool.wait_ge(hid_hi, u + 1)
                if u >= 2:
                    pool.wait_ge(downed, 4 * (u - 1))
                nc.gpsimd.tensor_tensor(hid_pair[u % 2][:, 1], hid[u % 2], hid_pair[u % 2][:, 0],
                                        ALU.subtract).then_inc(hid_lo, 1)

        @block.tensor
        def _(pe):
            m.ln_turn(pe, ln, tiles, 0)
            pe.wait_ge(ln["lo"], 4)
            pe.wait_ge(gate_lo, 1)
            for T in tiles:
                for c in range(C):
                    for i, (a, w) in enumerate(PASSES):
                        last = nc.tensor.matmul(bank(4, E * T, E * T + E), hT[:, a, c, P * T:P * T + P],
                                                gate[:, w, c], start=(c == 0 and i == 0),
                                                stop=(c == C - 1 and i == 2))
            last.then_inc(gated, 1)

            def expert_up(u):
                half, e = u // E, u % E
                if u >= 2:
                    pe.wait_ge(geled, 2 * (u - 1))
                for ic in range(2):
                    for c in range(C):
                        for i, (a, w) in enumerate(PASSES):
                            last = nc.tensor.matmul(bank(2 * (u % 2) + ic), w_up[:, a, e, c, ic * P:(ic + 1) * P],
                                                    hT[:, w, c, 512 * half:512 * half + 512],
                                                    start=(c == 0 and i == 0), stop=(c == C - 1 and i == 2))
                    last.then_inc(upped, 1)

            def expert_down(u):
                e = u % E
                pe.wait_ge(hid_lo, u + 1)
                for t in range(4):
                    if u >= 1:
                        pe.wait_ge(added, summed_rows(u - 1, t))
                    elif t == 0:
                        pe.wait_ge(s_route, 2)
                    for c in range(2):
                        for i, (a, w) in enumerate(PASSES):
                            last = nc.tensor.matmul(bank(4 + t, 0, 256),
                                                    hid_pair[u % 2][:, a, c, P * t:P * t + P], w_down[:, w, e, c],
                                                    start=(c == 0 and i == 0), stop=(c == 1 and i == 2))
                    last.then_inc(downed, 1)

            expert_up(0)
            for u in range(2 * E):
                if u + 1 < 2 * E:
                    expert_up(u + 1)
                expert_down(u)

        @block.scalar
        def _(act):
            act.wait_ge(s_vec, 64)
            act.wait_ge(s_gate, 16)
            nc.scalar.activation(gate[:, 0].rearrange("p c e -> p (c e)"), gate32, ACT.Copy, scale=WS).then_inc(gate_hi, 1)
            m.ln_hi(act, ln, 0, 2, ln_gain, ln_shift)
            act.wait_ge(s_route, 2)
            nc.scalar.activation(raw, logit, ACT.Exp, scale=1.0 / WS).then_inc(s_exp, 1)
            act.wait_ge(s_route, 8)
            nc.scalar.activation(comb, tmp, ACT.Exp).then_inc(s_exp, 1)
            for u in range(2 * E):
                e = u % E
                if u >= 2:
                    act.wait_ge(hid_lo, u - 1)
                for ic in range(2):
                    act.wait_ge(upped, 2 * u + ic + 1)
                    nc.scalar.activation(hid[u % 2][:, ic], bank(2 * (u % 2) + ic), ACT.Gelu, scale=1.0 / WS,
                                         bias=up_bias[:, 2 * e + ic:2 * e + ic + 1]).then_inc(geled, 1)
                act.wait_ge(geled, 2 * u + 2)
                if u >= 2:
                    act.wait_ge(downed, 4 * (u - 1))
                nc.scalar.activation(hid_pair[u % 2][:, 0], hid[u % 2], ACT.Copy).then_inc(hid_hi, 1)

        @block.vector
        def _(dve):
            route = [0]

            def step(ins):
                route[0] += 1
                ins.then_inc(s_route, 1)
                dve.wait_ge(s_route, route[0])

            m.ln_stats(dve, ln, tiles, m.h)
            dve.wait_ge(gate_hi, 1)
            nc.vector.scalar_tensor_tensor(out=gate[:, 1].rearrange("p c e -> p (c e)"), in0=gate32, scalar=WS,
                                           in1=gate[:, 0].rearrange("p c e -> p (c e)"), op0=ALU.mult,
                                           op1=ALU.subtract).then_inc(gate_lo, 1)
            m.ln_apply(dve, ln, tiles, m.h)
            dve.wait_ge(s_vec, 64)
            m.ln_lo(dve, ln, 0, 2, ln_gain, ln_shift)

            def each(v):
                return v.unsqueeze(2).broadcast_to([P, NT, E])
            dve.wait_ge(gated, 1)
            lg = bank(4, 0, NT * E).rearrange("p (t e) -> p t e", t=NT)
            step(nc.vector.tensor_reduce(tmax, lg, AX.X, ALU.max))
            step(nc.vector.tensor_tensor(logit, lg, each(tmax), ALU.subtract))
            dve.wait_ge(s_exp, 1)
            step(nc.vector.tensor_reduce(tsum, raw, AX.X, ALU.add))
            step(nc.vector.reciprocal(tsum, tsum))
            step(nc.vector.tensor_tensor(raw, raw, each(tsum), ALU.mult))
            step(nc.vector.tensor_reduce(tmax, raw, AX.X, ALU.max))
            step(nc.vector.tensor_tensor(tmp, raw, each(tmax), ALU.subtract))
            step(nc.vector.memset(rank, 0.0))
            dve.wait_ge(s_exp, 2)
            for j in range(E):
                for lo, hi, op in ((0, j, ALU.is_gt), (j + 1, E, ALU.is_ge)):
                    if lo == hi:
                        continue
                    rival = raw[:, :, j:j + 1].broadcast_to([P, NT, hi - lo])
                    step(nc.vector.tensor_tensor(tmp[:, :, lo:hi], rival, raw[:, :, lo:hi], op))
                    step(nc.vector.tensor_tensor(rank[:, :, lo:hi], rank[:, :, lo:hi], tmp[:, :, lo:hi], ALU.add))
            step(nc.vector.tensor_scalar(rank, rank, 1.5, None, ALU.is_lt))
            step(nc.vector.tensor_tensor(comb, comb, rank, ALU.mult))
            step(nc.vector.tensor_reduce(tsum, comb, AX.X, ALU.add))
            step(nc.vector.reciprocal(tsum, tsum))
            step(nc.vector.tensor_tensor(comb, comb, each(tsum), ALU.mult))
            step(nc.vector.tensor_scalar(logit, comb, 1.0 / WS, None, ALU.mult))

            dve.wait_ge(s_ready, 1)
            for u in range(2 * E):
                half, e = u // E, u % E
                for t in range(4):
                    T = 4 * half + t
                    if e:
                        dve.wait_ge(added, summed_rows(u - 1, t))
                    nc.vector.scalar_tensor_tensor(out=x[:, T], in0=down_bias[:, e], scalar=comb[:, T, e:e + 1],
                                                   in1=x[:, T], op0=ALU.mult, op1=ALU.add).then_inc(added, 1)
                for t in range(4):
                    T = 4 * half + t
                    dve.wait_ge(downed, 4 * u + t + 1)
                    dve.wait_ge(added, biased_rows(u, t))
                    nc.vector.scalar_tensor_tensor(out=x[:, T], in0=bank(4 + t, 0, 256),
                                                   scalar=logit[:, T, e:e + 1], in1=x[:, T], op0=ALU.mult,
                                                   op1=ALU.add).then_inc(added, 1)


PARTS = (layer0_attention, layer0_ffn, layer1_ctx_attention, layer1_attention, layer1_moe)


def kernel(**inputs):
    import concourse.bacc as _bacc
    from concourse.bass_utils import run_bass_kernel_spmd as _run

    nc = _bacc.Bacc("TRN2", target_bir_lowering=False, num_devices=1)
    arrays, io = {}, {}
    for name, value in {**inputs, "const": shape_constants()}.items():
        a = np.ascontiguousarray(value)
        arrays[f"in_{name}"] = a
        io[name] = nc.dram_tensor(f"in_{name}", a.shape, mybir.dt.from_np(a.dtype), kind="ExternalInput").ap()
    out = nc.dram_tensor("out_0", (B, S, D), F32, kind="ExternalOutput").ap()
    build(nc, io, out)
    r = _run(nc, [arrays], core_ids=[0])
    return r.results[0]["out_0"]
```
